# Optimizing a Trainium2 kernel written in Bass

```python
import numpy as np
import jax
import jax.numpy as jnp

def _softmax(x, axis=-1):
    return jax.nn.softmax(x, axis=axis)

def _gelu(x):
    return jax.nn.gelu(x, approximate=True)

def _silu(x):
    return jax.nn.silu(x)

def _sigmoid(x):
    return jax.nn.sigmoid(x)

def _layernorm(x, axis=-1, eps=1e-05):
    m = jnp.mean(x, axis=axis, keepdims=True)
    v = jnp.var(x, axis=axis, keepdims=True)
    return (x - m) / jnp.sqrt(v + eps)

def _scatter_add(tgt, idx, src, axis=0):
    return tgt.at[idx].add(src)

def _segment_sum(src, seg, n):
    return jax.ops.segment_sum(src, seg, n)
kernel_name = 'mk_xattn_ffn_d1_seqx_r4_8ee709'

def setup_inputs(seed: int=0):
    np.random.seed(seed)
    _w = jnp.asarray

    def _rec_inputs():
        import jax
        import jax.numpy as jnp
        _rk = jax.random.key(seed)
        x = -0.0002928 + 1 * jax.random.normal(jax.random.fold_in(_rk, 1), (1, 2048, 256), jnp.float32)
        _lenS = 2048 - jax.random.randint(jax.random.fold_in(_rk, 7), (1,), 0, max(1, 2048 // 4) + 1, jnp.int32)
        _lenS2 = 1601 - jax.random.randint(jax.random.fold_in(_rk, 8), (1,), 0, max(1, 1601 // 4) + 1, jnp.int32)
        _ctx_1024P = jax.random.normal(jax.random.fold_in(_rk, 11), (1, 16, 256), jnp.float32)
        _ctx_1024c = jax.random.dirichlet(jax.random.fold_in(_rk, 511), 0.3 * jnp.ones((16,), jnp.float32), (1, 1601))
        _ctx_1024t = jnp.einsum('bsk,bkd->bsd', _ctx_1024c, _ctx_1024P)
        _ctx_1024t = _ctx_1024t * jax.lax.rsqrt(jnp.mean(jnp.square(_ctx_1024t)) + 1e-12) * 0.953939
        ctx_1024 = -1.39393e-06 + 0.999914 * (_ctx_1024t + 0.3 * jax.random.normal(jax.random.fold_in(_rk, 611), (1, 1601, 256), jnp.float32))
        _validS = jnp.arange(2048)[None, :] < _lenS[:, None]
        _validS2 = jnp.arange(1601)[None, :] < _lenS2[:, None]
        _causal = jnp.tril(jnp.ones((2048, 2048), dtype=bool))
        mask_BxS2_ik0 = jnp.where(jnp.broadcast_to(_validS2[:, :], (1, 1601)), 0, 1).astype(jnp.int32)
        return (x, ctx_1024, mask_BxS2_ik0)
    x, ctx_1024, mask_BxS2_ik0 = _rec_inputs()

    def _L0_xattn_setup():
        import jax, jax.numpy as jnp
        import numpy as np
        D_MODEL = 256
        NUM_HEADS = 16
        D_K = D_MODEL // NUM_HEADS
        key = jax.random.key(seed)
        ks = jax.random.split(key, 10)
        B, Sq, Sk, D = (2, 512, 512, D_MODEL)
        scale = 1.0 / np.sqrt(D)
        mask = jax.random.randint(ks[3], (B, Sk), 0, 2, dtype=jnp.int32)
        mask = mask.at[:, :4].set(1)
        return {'query': jax.random.normal(ks[0], (B, Sq, D), jnp.float32), 'key': jax.random.normal(ks[1], (B, Sk, D), jnp.float32), 'value': jax.random.normal(ks[2], (B, Sk, D), jnp.float32), 'mask': mask, 'Wq': jax.random.normal(ks[4], (D, D), jnp.float32) * scale, 'Wk': jax.random.normal(ks[5], (D, D), jnp.float32) * scale, 'Wv': jax.random.normal(ks[6], (D, D), jnp.float32) * scale, 'Wo': jax.random.normal(ks[7], (D, D), jnp.float32) * scale, 'Wg': jax.random.normal(ks[8], (D, D), jnp.float32) * scale, 'bg': jax.random.normal(ks[9], (D,), jnp.float32) * 0.02}
    _L0_xattn_all = _L0_xattn_setup()
    _L0_xattn_in = {k: v for k, v in _L0_xattn_all.items() if k in ('Wq', 'Wk', 'Wv', 'Wo', 'Wg', 'bg')}
    del _L0_xattn_all

    def _L0_ffn_setup():
        import jax, jax.numpy as jnp
        import numpy as np
        TOP_K = 2
        key = jax.random.key(seed)
        k_x, k_g, k_w1, k_w2, k_w3 = jax.random.split(key, 5)
        B, S, D, H, E = (2, 128, 256, 128, 8)
        x = jax.random.normal(k_x, (B, S, D), dtype=jnp.float32)
        gate_w = jax.random.normal(k_g, (D, E), dtype=jnp.float32) * D ** (-0.5)
        w1 = jax.random.normal(k_w1, (E, D, H), dtype=jnp.float32) * 0.02
        w2 = jax.random.normal(k_w2, (E, H, D), dtype=jnp.float32) * 0.02
        w3 = jax.random.normal(k_w3, (E, D, H), dtype=jnp.float32) * 0.02
        return {'x': x, 'gate_w': gate_w, 'w1': w1, 'w2': w2, 'w3': w3}
    _L0_ffn_all = _L0_ffn_setup()
    _L0_ffn_in = {k: v for k, v in _L0_ffn_all.items() if k in ('gate_w', 'w1', 'w2', 'w3')}
    del _L0_ffn_all
    return {'x': x, 'ctx_1024': ctx_1024, 'mask_BxS2_ik0': mask_BxS2_ik0, 'L0_xattn_Wq': _L0_xattn_in['Wq'], 'L0_xattn_Wk': _L0_xattn_in['Wk'], 'L0_xattn_Wv': _L0_xattn_in['Wv'], 'L0_xattn_Wo': _L0_xattn_in['Wo'], 'L0_xattn_Wg': _L0_xattn_in['Wg'], 'L0_xattn_bg': _L0_xattn_in['bg'], 'L0_ffn_gate_w': _L0_ffn_in['gate_w'], 'L0_ffn_w1': _L0_ffn_in['w1'], 'L0_ffn_w2': _L0_ffn_in['w2'], 'L0_ffn_w3': _L0_ffn_in['w3']}

def reference(x, ctx_1024, mask_BxS2_ik0, L0_xattn_Wq, L0_xattn_Wk, L0_xattn_Wv, L0_xattn_Wo, L0_xattn_Wg, L0_xattn_bg, L0_ffn_gate_w, L0_ffn_w1, L0_ffn_w2, L0_ffn_w3):
    import jax
    import jax.numpy as jnp

    def _L0_xattn_ref(query, key, value, mask, Wq, Wk, Wv, Wo, Wg, bg):
        import jax, jax.numpy as jnp
        import numpy as np
        D_MODEL = 256
        NUM_HEADS = 16
        D_K = D_MODEL // NUM_HEADS
        B, Sq, D = query.shape
        Sk = key.shape[1]
        H, dk = (NUM_HEADS, D_K)
        q = (query @ Wq.T).reshape(B, Sq, H, dk).transpose(0, 2, 1, 3)
        k = (key @ Wk.T).reshape(B, Sk, H, dk).transpose(0, 2, 1, 3)
        v = (value @ Wv.T).reshape(B, Sk, H, dk).transpose(0, 2, 1, 3)
        scores = jnp.einsum('bhqd,bhkd->bhqk', q, k) / jnp.sqrt(jnp.float32(dk))
        neg_inf = jnp.float32(-jnp.inf)
        scores = jnp.where(mask[:, None, None, :] == 0, neg_inf, scores)
        future = jnp.triu(jnp.ones((Sq, Sk), dtype=bool), k=1)
        scores = jnp.where(future[None, None, :, :], neg_inf, scores)
        attn = jax.nn.softmax(scores, axis=-1)
        attn = jnp.nan_to_num(attn, nan=0.0)
        context = jnp.einsum('bhqk,bhkd->bhqd', attn, v)
        context = context.transpose(0, 2, 1, 3).reshape(B, Sq, D)
        gate = jax.nn.sigmoid(query @ Wg.T + bg)
        output = gate * context @ Wo.T
        return output

    def _L0_ffn_ref(x, gate_w, w1, w2, w3):
        import jax, jax.numpy as jnp
        import numpy as np
        TOP_K = 2
        B, S, D = x.shape
        E = gate_w.shape[1]
        xf = x.reshape(B * S, D)
        T = B * S
        logits = xf @ gate_w
        scores = jax.nn.softmax(logits, axis=-1)
        top_scores, top_idx = jax.lax.top_k(scores, TOP_K)
        scale = jnp.zeros((T, E), dtype=x.dtype).at[jnp.arange(T)[:, None], top_idx].set(top_scores)
        xs = scale.T[:, :, None] * xf[None, :, :]
        h = jax.nn.silu(jnp.einsum('etd,edh->eth', xs, w1)) * jnp.einsum('etd,edh->eth', xs, w3)
        y = jnp.einsum('eth,ehd->etd', h, w2)
        out = y.sum(axis=0)
        return out.reshape(B, S, D)
    x = x + _L0_xattn_ref(_layernorm(x, axis=-1), ctx_1024, ctx_1024, mask_BxS2_ik0, L0_xattn_Wq, L0_xattn_Wk, L0_xattn_Wv, L0_xattn_Wo, L0_xattn_Wg, L0_xattn_bg)
    x = x + _L0_ffn_ref(_layernorm(x, axis=-1), L0_ffn_gate_w, L0_ffn_w1, L0_ffn_w2, L0_ffn_w3)
    return x

_drawn_inputs = setup_inputs


def setup_inputs(seed=0):
    import zlib

    import numpy as np

    out = dict(_drawn_inputs(seed))
    spreads = {}
    factors = {'L0_xattn_bg': 8.0,
     'L0_ffn_gate_w': 8.0,
     'L0_ffn_w1': 8.0,
     'L0_ffn_w2': 8.0,
     'L0_ffn_w3': 8.0}
    for name, (base, spread) in spreads.items():
        noise = np.random.default_rng([zlib.crc32(name.encode()), seed]).standard_normal(out[name].shape)
        drawn = base * np.exp(spread * noise) if base else spread * noise
        out[name] = jnp.asarray(drawn.astype(out[name].dtype))
    for name, factor in factors.items():
        out[name] = (out[name] * factor).astype(out[name].dtype)
    return out
```

```python
from contextlib import ExitStack

import numpy as np

import concourse.bass as bass
from concourse import mybir

F32 = mybir.dt.float32
BF16 = mybir.dt.bfloat16
I32 = mybir.dt.int32
ALU = mybir.AluOpType
ACT = mybir.ActivationFunctionType
AX_X = mybir.AxisListType.X

P = 128
TOK, KEYS, D, H, DK = 2048, 1601, 256, 16, 16
E, HID = 8, 128
CH = 512
NC = TOK // CH
TPC = CH // P
NT = TOK // P
KT = (KEYS + P - 1) // P
KD = D // P
KP = 1602
G = H // 4
RING, RING0 = 3, 3
ST_BANKS = 3
NSLOT = 2
MASKED = -1.0e30
FLOOR = -1.0e20
TINY = 1.0e-30
EPS = 1e-5
VW = DK + 1
Y_BANKS = (0, 1, 2, 6)
Q_PARTS = (0, 0, 0, 1, 1, 2)
K_PARTS = (0, 1, 2, 0, 1, 0)
ROW_MASK = len(Q_PARTS) * DK
ROW_MAX = ROW_MASK + 1
ROWS = ROW_MAX + 2


TWO_ONES = float(np.uint32(0x3F803F80).view(np.float32))


def key_tiles(c):
    return min(TPC * (c + 1), KT)


def key_rows(j):
    return min(P, KEYS - P * j)


def max_pieces(n):
    c, out = n // G, []
    for h in range(4):
        for qt in range(TPC):
            i = TPC * c + qt
            seen = min(P * (i + 1), KEYS)
            for k0 in range(0, seen, CH):
                w = min(CH, seen - k0)
                out.append((qt, h, k0, w, i < KT and k0 + w == seen))
    return out


def make_plan():
    plan, due = [], []

    def later(unit, *events):
        due.extend((unit, e) for e in events)

    def emit_due(unit):
        now = [e for u, e in due if u <= unit]
        due[:] = [(u, e) for u, e in due if u > unit]
        plan.extend(now)

    for c in range(NC):
        plan.extend([("kq", "k", 0, c), ("kq", "k", 1, c), ("kload", c), ("stat", 0, c), ("sqrt", 0, c), ("norm", 0, c)])
        plan.extend([("v", t) for t in range(4 * c, min(4 * c + 2, KT))])
        plan.extend([("xT", 0, c, 0), ("xT", 0, c, 1), ("kq", "q", 0, c), ("kq", "q", 1, c)])
        if c < 2:
            plan.append(("qload", c))
        plan.extend([("gate", c, 0), ("gate", c, 1), ("sigmoid", c)])
        plan.extend([("v", t) for t in range(4 * c + 2, min(4 * c + 4, KT))])
        if c == 3:
            plan.append(("prologue_end",))
    for n in (0, 1):
        plan.extend([("mx", n, k) for k in range(len(max_pieces(n)))] + [("mred", n)])
    plan.extend([("mT", 0), ("mT", 1)])

    units = [(n, j) for n in range(NC * G) for j in range(key_tiles(n // G))]
    last_unit = {n: u for u, (n, _) in enumerate(units)}
    first_unit = {}
    for u, (n, _) in enumerate(units):
        first_unit.setdefault(n, u)

    def after_chunk(c, u):
        later(u + 2, ("gT", c, 0), ("gT", c, 1))
        later(u + 3, ("wo", c, 0), ("wo", c, 1), ("stat", 1, c))
        later(u + 4, ("sqrt", 1, c), ("norm", 1, c))
        later(u + 5, ("xT", 1, c, 0), ("xT", 1, c, 1))
        later(u + 6, ("logits", c), ("rexp", c), ("rank", c))
        later(u + 7, ("sT", c))

    for u, (n, j) in enumerate(units):
        todo = []
        if n + 2 < NC * G:
            count = len(max_pieces(n + 2))
            width = last_unit[n] - first_unit[n] + 1
            at = u - first_unit[n]
            todo = [("mx", n + 2, k) for k in range(count * at // width, count * (at + 1) // width)]
        for h in range(4):
            plan.append(("st", u, n, j, h))
            plan.extend(todo[len(todo) * h // 4:len(todo) * (h + 1) // 4])
            if h == 1 and u > 0 and units[u - 1][0] == n - 1 and u > 1:
                pass
        if u > 0:
            plan.append(("pv", u - 1, *units[u - 1]))
        emit_due(u)
        if u > 0 and units[u - 1][0] != n:
            m = n - 1
            later(u + 1, ("ocopy", m), ("oT", m))
            if m % G == G - 1:
                after_chunk(m // G, u)
                if m // G + 2 < NC:
                    plan.append(("qload", m // G + 2))
                if m // G == 2:
                    later(u + 1, ("sload", 0))
        if u == last_unit[n] and n + 2 < NC * G:
            plan.append(("mred", n + 2))
            later(u + 2, ("mT", n + 2))
    u = len(units)
    plan.append(("pv", u - 1, *units[u - 1]))
    later(u, ("ocopy", NC * G - 1), ("oT", NC * G - 1))
    after_chunk(NC - 1, u)
    for c in range(NC):
        for e in range(E):
            if (c, e) == (0, 1):
                later(u, ("sload", 1))
            plan.extend([("a", c, e), ("b", c, e), ("h", c, e)])
            emit_due(u)
            u += 1
            if e:
                plan.append(("y", c, e - 1))
        plan.append(("y", c, E - 1))
        plan.append(("out", c))
        if c + 2 < NC:
            plan.append(("sload", c + 2))
    return plan, units


RING_ITEMS = ("kq", "v", "xT", "gate", "mx", "mT", "oT", "gT", "wo", "logits", "sT", "a", "b")


def build(nc, x, ctx_t, mask, wq_t, wk_t, wv_t, wo_t, wg_t, bg, gate_w, w1, w2, w3, out):
    plan, units = make_plan()
    ring_at = {e: i for i, e in enumerate([e for e in plan if e[0] in RING_ITEMS])}
    kq_at = {e: i for i, e in enumerate([e for e in plan if e[0] == "kq"])}
    st_at = {(e[1], e[4]): i for i, e in enumerate([e for e in plan if e[0] == "st"])}
    last_st = {}
    for u, (n, _) in enumerate(units):
        last_st[n // G] = st_at[(u, 3)]
    prologue_items = max(i for e, i in ring_at.items() if e[0] in ("kq", "v", "gate")) + 1

    with ExitStack() as ctx:
        def sb(name, shape, dt, stack=ctx):
            return stack.enter_context(nc.sbuf_tensor(name, shape, dt))

        def sem(name):
            return ctx.enter_context(nc.semaphore(name))

        def scratch(name, shape, dt):
            return nc.dram_tensor(name, shape, dt, kind="Internal").ap()

        k_parts = scratch("k_parts", (3, D, KEYS), BF16)
        q_parts = scratch("q_parts", (3, D, TOK), BF16)
        s_dram = scratch("s_dram", (E, TOK), F32)

        x_sb = sb("x_sb", [P, NT, D], F32)
        gate_sb = sb("gate_sb", [P, NC, TPC * D], F32)
        kaug = sb("kaug", [P, H, KP], BF16)
        qaug = sb("qaug", [P, 2, H, CH], BF16)
        vaug = sb("vaug", [P, KT * H * VW + 16], F32)
        probs = sb("probs", [P, NSLOT, 4, CH], F32)
        o_sb = sb("o_sb", [P, CH], F32)
        att_sb = sb("att_sb", [P, TPC, D], F32)
        att_t = sb("att_t", [P, KD, CH], F32)
        xn_sb = sb("xn_sb", [P, TPC, D], F32)
        wo_sb = sb("wo_sb", [P, KD, D], F32)
        gw_sb = sb("gw_sb", [P, KD, E], F32)
        ident = sb("ident", [P, P], F32)
        ident_b = sb("ident_b", [P, P], BF16)
        zero_b = sb("zero_b", [P, P], BF16)
        tri_kq = sb("tri_kq", [P, P], BF16)
        tri_qk = sb("tri_qk", [P, P], BF16)
        lower = sb("lower", [P, E, E], F32)
        ones_f = sb("ones_f", [P, E, E], F32)
        pmax = sb("pmax", [P, 2, TPC, 4, 4], F32)
        rmax = sb("rmax", [P, 2, TPC * 4], F32)
        nmax = sb("nmax", [P, 2, TPC * 4], F32)
        nmax_b = sb("nmax_b", [P, 2, TPC, 2, 4], BF16)
        m_row = sb("m_row", [8, 2, CH], BF16)
        stat6 = sb("stat6", [P, TPC, 6], F32)
        stat2 = sb("stat2", [P, TPC, 2], F32)
        var_e = sb("var_e", [P, TPC], F32)
        std = sb("std", [P, TPC], F32)
        rstd = sb("rstd", [P, TPC], F32)
        rsum = sb("rsum", [P, TPC, 4], F32)
        rinv = sb("rinv", [P, TPC, 4], F32)
        r_max = sb("r_max", [P, TPC], F32)
        r_log = sb("r_log", [P, TPC, E], F32)
        r_exp = sb("r_exp", [P, TPC, E], F32)
        r_sum = sb("r_sum", [P, TPC], F32)
        r_inv = sb("r_inv", [P, TPC], F32)
        r_prob = sb("r_prob", [P, TPC, E], F32)
        r_gt = sb("r_gt", [P, TPC, E, E], F32)
        r_eq = sb("r_eq", [P, TPC, E, E], F32)
        r_rank = sb("r_rank", [P, TPC, E], F32)
        scale_sb = sb("scale_sb", [P, TPC, E], F32)
        sT_sb = sb("sT_sb", [E, CH], F32)
        with ExitStack() as early:
            ctx_sb = sb("ctx_sb", [P, KD, KEYS], F32, early)
            wq_sb = sb("wq_sb", [P, KD, D], F32, early)
            wk_sb = sb("wk_sb", [P, KD, D], F32, early)
            wv_sb = sb("wv_sb", [P, KD, D], F32, early)
            wg_sb = sb("wg_sb", [P, KD, D], F32, early)
            xn_t = sb("xn_t", [P, 2, KD, CH], F32, early)
            bg_sb = sb("bg_sb", [P, D], F32, early)
            mask_i = sb("mask_i", [1, KEYS], I32, early)
        w1_sb = sb("w1_sb", [P, E, KD, HID], F32)
        w3_sb = sb("w3_sb", [P, E, KD, HID], F32)
        w2_sb = sb("w2_sb", [P, E, D], F32)
        stage_words = probs[:, :, :, :].rearrange("p s h q -> p (s h q)")
        stage = [stage_words[:, 768 * s:768 * (s + 1)].bitcast(BF16).rearrange("p (a q) -> p a q", a=3) for s in range(2)]
        rest = [stage_words[:, 2048 + CH * s:2048 + CH * (s + 1)] for s in range(2)]
        late = kaug[:, :, :].rearrange("p h k -> p (h k)").bitcast(F32)
        u_sb = [late[:, CH * s:CH * (s + 1)] for s in (0, 1)]
        g_sb = [late[:, CH * s:CH * (s + 1)] for s in (2, 3)]
        v_sb = [late[:, CH * s:CH * (s + 1)] for s in (4, 5)]
        h_sb = [late[:, CH * s:CH * (s + 1)] for s in (6, 7)]
        scale_bc = [qaug[:, s, :, :].rearrange("p h q -> p (h q)").bitcast(F32).rearrange("p (e q) -> p e q", e=E)
                    for s in range(2)]
        vflat = vaug[:, 0:KT * H * VW].rearrange("p (t h w) -> p t h w", t=KT, h=H)
        bias_row = att_t[0:1, :, :].rearrange("p a q -> p (a q)").bitcast(BF16)[:, 0:KEYS]

        psum = [ctx.enter_context(nc.psum_tensor(f"bank{i}", [P, CH], F32)) for i in range(8)]

        def ring_bank(e):
            return psum[RING0 + ring_at[e] % RING]

        ld = {k: sem(f"ld_{k}") for k in ("wk", "wq", "wv", "wg", "bg", "wo", "gw", "mask", "w1", "w3", "w2")}
        ld_ctx = [sem(f"ld_ctx{i}") for i in range(NC)]
        ld_x = [sem(f"ld_x{i}") for i in range(NC)]
        consts = sem("consts")
        aug_rows = sem("aug_rows")
        v_ones = sem("v_ones")
        bias_ready = sem("bias_ready")
        bias_landed = sem("bias_landed")
        ring_full = sem("ring_full")
        ring_read = sem("ring_read")
        hi_ready = sem("hi_ready")
        mid_ready = sem("mid_ready")
        lo_ready = sem("lo_ready")
        parts_out = [sem(f"parts_out{i}") for i in range(2)]
        k_landed = [sem(f"k_landed{i}") for i in range(NC)]
        q_landed = [sem(f"q_landed{i}") for i in range(NC)]
        var_ready = sem("var_ready")
        std_ready = sem("std_ready")
        xn_ready = sem("xn_ready")
        gate_ready = sem("gate_ready")
        st_full = sem("st_full")
        exp_done = sem("exp_done")
        pv_done = sem("pv_done")
        mx_reduced = sem("mx_reduced")
        nm_ready = sem("nm_ready")
        nm_step = sem("nm_step")
        m_landed = [sem(f"m_landed{i}") for i in range(4)]
        o_copied = sem("o_copied")
        gated = sem("gated")
        r_log_ready = sem("r_log_ready")
        r_exp_ready = sem("r_exp_ready")
        scale_ready = sem("scale_ready")
        s_stored = [sem(f"s_stored{i}") for i in range(NC)]
        s_landed = [sem(f"s_landed{i}") for i in range(NC)]
        silu_done = sem("silu_done")
        h_ready = sem("h_ready")
        y_full = sem("y_full")
        y_added = sem("y_added")
        out_done = sem("out_done")
        dve_step = sem("dve_step")
        block = ctx.enter_context(nc.Block())

        @block.sync
        def _(sp):
            def tiles(w):
                return w.rearrange("(a p) n -> p a n", p=P)

            sp.dma_start(wk_sb[:, :, :], tiles(wk_t)).then_inc(ld["wk"], 16)
            for c in range(NC):
                k0, k1 = CH * c, min(CH * (c + 1), KEYS)
                sp.dma_start(ctx_sb[:, :, k0:k1], tiles(ctx_t)[:, :, k0:k1]).then_inc(ld_ctx[c], 16)
            for name, dst, src in (("wq", wq_sb, wq_t), ("wg", wg_sb, wg_t), ("wo", wo_sb, wo_t), ("gw", gw_sb, gate_w)):
                sp.dma_start(dst[:, :, :], tiles(src)).then_inc(ld[name], 16)
            for e in plan:
                kind = e[0]
                if kind == "kq":
                    i, (_, what, m, c) = kq_at[e], e
                    w = min(CH, KEYS - CH * c) if what == "k" else CH
                    parts = k_parts if what == "k" else q_parts
                    sp.wait_ge(hi_ready, i + 1)
                    sp.wait_ge(mid_ready, i + 1)
                    sp.wait_ge(lo_ready, i + 1)
                    sp.dma_start(parts[:, P * m:P * (m + 1), CH * c:CH * c + w].rearrange("a p q -> p a q"),
                                 stage[i % 2][:, :, 0:w]).then_inc(parts_out[i % 2], 16)
                elif kind in ("kload", "qload"):
                    c, what = e[1], kind[0]
                    i = kq_at[("kq", what, 1, c)]
                    sp.wait_ge(parts_out[i % 2], 16 * (i // 2 + 1))
                    sp.wait_ge(parts_out[(i - 1) % 2], 16 * ((i - 1) // 2 + 1))
                    if what == "q" and c >= 2:
                        sp.wait_ge(st_full, last_st[c - 2] + 1)
                    w = min(CH, KEYS - CH * c) if what == "k" else CH
                    for r in range(len(Q_PARTS)):
                        if what == "k":
                            dst = kaug[DK * r:DK * (r + 1), :, CH * c:CH * c + w]
                            src = k_parts[K_PARTS[r], :, CH * c:CH * c + w]
                        else:
                            dst = qaug[DK * r:DK * (r + 1), c % 2, :, :]
                            src = q_parts[Q_PARTS[r], :, CH * c:CH * c + w]
                        sp.dma_start(dst, src.rearrange("(h d) q -> d h q", d=DK)
                                     ).then_inc((k_landed if what == "k" else q_landed)[c], 16)
                    if what == "k" and c == 0:
                        sp.wait_ge(aug_rows, 1)
                        sp.wait_ge(bias_ready, 1)
                        sp.dma_start(kaug[ROW_MASK:ROW_MASK + 1, :, 0:KEYS],
                                     bias_row.unsqueeze(1).to_broadcast([1, H, KEYS])).then_inc(bias_landed, 16)
                elif kind == "mT":
                    n = e[1]
                    c, g = n // G, n % G
                    sp.wait_ge(ring_read, ring_at[e] + 1)
                    sp.wait_ge(aug_rows, 2)
                    for part in range(2):
                        sp.dma_start(qaug[ROW_MAX + part:ROW_MAX + part + 1, c % 2, 4 * g:4 * g + 4, :],
                                     m_row[4 * part:4 * part + 4, n % 2, :]).then_inc(m_landed[n % 4], 16)
                elif kind == "prologue_end":
                    sp.wait_ge(ring_full, prologue_items)
                    sp.wait_ge(ring_read, prologue_items)
                    sp.dma_start(w1_sb[:, :, :, :], w1.rearrange("e (a p) h -> p e a h", p=P)).then_inc(ld["w1"], 16)
                    sp.dma_start(w3_sb[:, :, :, :], w3.rearrange("e (a p) h -> p e a h", p=P)).then_inc(ld["w3"], 16)
                    sp.dma_start(w2_sb[:, :, :], w2.rearrange("e h d -> h e d")).then_inc(ld["w2"], 16)
                elif kind == "sT":
                    c = e[1]
                    sp.wait_ge(ring_read, ring_at[e] + 1)
                    sp.dma_start(s_dram[:, CH * c:CH * (c + 1)], sT_sb[:, :]).then_inc(s_stored[c], 16)
                elif kind == "sload":
                    c = e[1]
                    sp.wait_ge(s_stored[c], 16)
                    if c == 0:
                        sp.wait_ge(st_full, last_st[2] + 1)
                    elif c == 1:
                        sp.wait_ge(st_full, last_st[3] + 1)
                    else:
                        sp.wait_ge(ring_read, ring_at[("b", c - 2, E - 1)] + 1)
                    sp.dma_start(scale_bc[c % 2], s_dram[:, CH * c:CH * (c + 1)].partition_broadcast(P)
                                 ).then_inc(s_landed[c], 16)
                elif kind == "out":
                    c = e[1]
                    sp.wait_ge(y_added, c + 1)
                    sp.dma_start(out.rearrange("(t p) d -> p t d", p=P)[:, TPC * c:TPC * (c + 1), :],
                                 x_sb[:, TPC * c:TPC * (c + 1), :]).then_inc(out_done, 16)
            sp.wait_ge(out_done, 16 * NC)

        @block.gpsimd
        def _(pool):
            def select(dst, src, pattern, base, mult, op, fill):
                return pool.affine_select(out=dst, in_=src, compare_op=op, fill=fill, base=base,
                                          pattern=pattern, channel_multiplier=mult)

            pool.memset(zero_b[:, :], 0.0).then_inc(consts, 1)
            pool.memset(ident[:, :], 0.0).then_inc(consts, 1)
            pool.memset(ones_f[:, :, :], 1.0).then_inc(consts, 1)
            pool.wait_ge(consts, 3)
            select(ident[:, :], ident[:, :], [[-1, P]], 0, 1, ALU.not_equal, 1.0).then_inc(consts, 1)
            select(ident_b[:, :], zero_b[:, :], [[-1, P]], 0, 1, ALU.not_equal, 1.0).then_inc(consts, 1)
            select(tri_kq[:, :], zero_b[:, :], [[1, P]], 0, -1, ALU.is_ge, MASKED).then_inc(consts, 1)
            select(tri_qk[:, :], zero_b[:, :], [[-1, P]], 0, 1, ALU.is_ge, MASKED).then_inc(consts, 1)
            select(lower[:, :, :], ones_f[:, :, :], [[1, E], [-1, E]], 0, 0, ALU.is_gt, 0.0).then_inc(consts, 1)
            pool.wait_ge(consts, 8)
            pool.memset(kaug[ROW_MASK:ROWS, :, :].rearrange("p h k -> p (h k)").bitcast(F32), TWO_ONES).then_inc(aug_rows, 1)
            pool.wait_ge(aug_rows, 1)
            pool.memset(qaug[ROW_MASK:ROWS, :, :, :].rearrange("p s h k -> p (s h k)").bitcast(F32), TWO_ONES).then_inc(aug_rows, 1)
            pool.wait_ge(aug_rows, 2)

            for e in plan:
                kind = e[0]
                if kind == "kq":
                    i, (_, what, m, c) = kq_at[e], e
                    w = min(CH, KEYS - CH * c) if what == "k" else CH
                    pool.wait_ge(ring_read, ring_at[e] + 1)
                    pool.wait_ge(mid_ready, i + 1)
                    pool.tensor_tensor(stage[i % 2][:, 2, 0:w], rest[i % 2][:, 0:w], stage[i % 2][:, 1, 0:w],
                                       ALU.subtract).then_inc(lo_ready, 1)
                elif kind == "mred":
                    n = e[1]
                    s = n % 2
                    view = nmax[:, s, :].rearrange("p (t h) -> p t h", t=TPC)
                    pool.wait_ge(mx_reduced, n + 1)
                    if n >= 2:
                        pool.wait_ge(ring_read, ring_at[("mT", n - 2)] + 1)
                    pool.tensor_scalar(nmax[:, s, :], rmax[:, s, :], FLOOR, -1.0, ALU.max, ALU.mult).then_inc(nm_step, 1)
                    pool.wait_ge(nm_step, 2 * n + 1)
                    pool.tensor_copy(nmax_b[:, s, :, 0, :], view).then_inc(nm_step, 1)
                    pool.wait_ge(nm_step, 2 * n + 2)
                    pool.tensor_tensor(nmax_b[:, s, :, 1, :], view, nmax_b[:, s, :, 0, :], ALU.subtract).then_inc(nm_ready, 1)
                elif kind == "oT":
                    n = e[1]
                    c, g = n // G, n % G
                    view = att_sb[:, :, 64 * g:64 * (g + 1)]
                    pool.wait_ge(ring_read, ring_at[e] + 1)
                    pool.wait_ge(gate_ready, c + 1)
                    pool.tensor_tensor(view, view,
                                       gate_sb[:, c, :].rearrange("p (t d) -> p t d", t=TPC)[:, :, 64 * g:64 * (g + 1)],
                                       ALU.mult).then_inc(gated, 1)

        @block.scalar
        def _(act):
            xv = x.rearrange("(t p) d -> p t d", p=P)
            act.dma_start(mask_i[:, :], mask).then_inc(ld["mask"], 16)
            act.dma_start(x_sb[:, 0:TPC, :], xv[:, 0:TPC, :]).then_inc(ld_x[0], 16)
            act.dma_start(wv_sb[:, :, :], wv_t.rearrange("(a p) n -> p a n", p=P)).then_inc(ld["wv"], 16)
            act.dma_start(bg_sb[:, :], bg.partition_broadcast(P)).then_inc(ld["bg"], 16)
            for c in range(1, NC):
                act.dma_start(x_sb[:, TPC * c:TPC * (c + 1), :], xv[:, TPC * c:TPC * (c + 1), :]).then_inc(ld_x[c], 16)
            norms = 0
            for e in plan:
                kind = e[0]
                if kind == "kq":
                    i, (_, what, m, c) = kq_at[e], e
                    w = min(CH, KEYS - CH * c) if what == "k" else CH
                    act.wait_ge(ring_read, ring_at[e] + 1)
                    act.activation(stage[i % 2][:, 1, 0:w], rest[i % 2][:, 0:w], ACT.Copy).then_inc(mid_ready, 1)
                elif kind == "sqrt":
                    norms += 1
                    act.wait_ge(var_ready, norms)
                    act.activation(std[:, :], var_e[:, :], ACT.Sqrt).then_inc(std_ready, 1)
                elif kind == "sigmoid":
                    c = e[1]
                    act.wait_ge(ring_read, ring_at[("gate", c, 1)] + 1)
                    act.activation(gate_sb[:, c, :], gate_sb[:, c, :], ACT.Sigmoid).then_inc(gate_ready, 1)
                elif kind == "st":
                    _, u, n, j, h = e
                    i = st_at[(u, h)]
                    off = max(0, P * (j - TPC * (n // G)))
                    rows = key_rows(j)
                    if i == 0:
                        for s in range(2):
                            act.wait_ge(parts_out[s], 16 * (len(kq_at) // 2))
                    act.wait_ge(st_full, i + 1)
                    if u >= NSLOT:
                        act.wait_ge(pv_done, u - NSLOT + 1)
                    act.activation(probs[0:rows, u % NSLOT, h, off:CH], psum[i % ST_BANKS][0:rows, off:CH], ACT.Exp,
                                   scale=DK ** -0.5).then_inc(exp_done, 1)
                elif kind == "rexp":
                    c = e[1]
                    act.wait_ge(r_log_ready, c + 1)
                    act.activation(r_exp[:, :, :], r_log[:, :, :], ACT.Exp).then_inc(r_exp_ready, 1)
                elif kind == "h":
                    _, c, ex = e
                    i = c * E + ex
                    act.wait_ge(ring_read, ring_at[("a", c, ex)] + 1)
                    if i >= 2:
                        act.wait_ge(h_ready, i - 1)
                    act.activation(g_sb[i % 2], u_sb[i % 2], ACT.Silu).then_inc(silu_done, 1)

        @block.vector
        def _(dve):
            steps = [0]

            def step(ins):
                ins.then_inc(dve_step, 1)
                steps[0] += 1
                dve.wait_ge(dve_step, steps[0])

            dve.memset(vaug[:, :], 1.0).then_inc(v_ones, 1)
            dve.memset(pmax[:, :, :, :, :], MASKED).then_inc(v_ones, 1)
            dve.wait_ge(ld["mask"], 16)
            dve.tensor_scalar(bias_row, mask_i[:, :], 0, MASKED, ALU.is_equal, ALU.mult).then_inc(bias_ready, 1)
            dve.wait_ge(v_ones, 2)
            norms = 0
            for e in plan:
                kind = e[0]
                if kind in RING_ITEMS:
                    dve.wait_ge(ring_full, ring_at[e] + 1)
                    bank = ring_bank(e)
                if kind == "kq":
                    i, (_, what, m, c) = kq_at[e], e
                    w = min(CH, KEYS - CH * c) if what == "k" else CH
                    if i >= 2:
                        dve.wait_ge(parts_out[i % 2], 16 * (i // 2))
                    dve.tensor_copy(stage[i % 2][:, 0, 0:w], bank[:, 0:w]).then_inc(hi_ready, 1)
                    dve.wait_ge(hi_ready, i + 1)
                    dve.tensor_tensor(rest[i % 2][:, 0:w], bank[:, 0:w], stage[i % 2][:, 0, 0:w],
                                      ALU.subtract).then_inc(ring_read, 1)
                elif kind == "v":
                    t = e[1]
                    r = key_rows(t)
                    dve.tensor_copy(vflat[0:r, t, :, 0:DK],
                                    bank[0:r, 0:D].rearrange("p (h d) -> p h d", h=H)).then_inc(ring_read, 1)
                elif kind == "stat":
                    _, second, c = e
                    if not second:
                        dve.wait_ge(ld_x[c], 16)
                    else:
                        dve.wait_ge(ring_read, ring_at[("wo", c, 1)] + 1)
                    for t in range(TPC):
                        last = dve.bn_stats(stat6[:, t, :], x_sb[:, TPC * c + t, :])
                    step(last)
                    for t in range(TPC):
                        last = dve.bn_aggr(stat2[:, t, :], stat6[:, t, :])
                    step(last)
                    dve.tensor_scalar(var_e[:, :], stat2[:, :, 1], EPS, None, ALU.add).then_inc(var_ready, 1)
                elif kind == "norm":
                    _, second, c = e
                    norms += 1
                    dve.wait_ge(std_ready, norms)
                    step(dve.reciprocal(rstd[:, :], std[:, :]))
                    if norms > 1:
                        before = ("xT", 0, c - 1, 1) if not second else ("xT", 1, c - 1, 1) if c else ("xT", 0, NC - 1, 1)
                        dve.wait_ge(ring_full, ring_at[before] + 1)
                    for t in range(TPC):
                        last = dve.tensor_scalar(xn_sb[:, t, :], x_sb[:, TPC * c + t, :], stat2[:, t, 0:1],
                                                 rstd[:, t:t + 1], ALU.subtract, ALU.mult)
                    last.then_inc(xn_ready, 1)
                elif kind == "xT":
                    _, second, c, half = e
                    if second:
                        dst = gate_sb[:, c, :].rearrange("p (a q) -> p a q", a=KD)
                        dve.wait_ge(gated, G * (c + 1))
                    else:
                        dst = xn_t[:, c % 2, :, :]
                        if c >= 2:
                            dve.wait_ge(ring_full, ring_at[("gate", c - 2, 1)] + 1)
                    dst = dst.rearrange("p a (t q) -> p t a q", q=P)[:, 2 * half:2 * half + 2, :, :]
                    dve.tensor_copy(dst, bank[:, :].rearrange("p (t a q) -> p t a q", t=2, a=KD)).then_inc(ring_read, 1)
                elif kind == "gate":
                    _, c, half = e
                    if (c, half) == (0, 0):
                        dve.wait_ge(ld["bg"], 16)
                    dve.tensor_tensor(gate_sb[:, c, CH * half:CH * (half + 1)].rearrange("p (t d) -> p t d", t=2),
                                      bank[:, :].rearrange("p (t d) -> p t d", t=2),
                                      bg_sb[:, :].unsqueeze(1).to_broadcast([P, 2, D]), ALU.add).then_inc(ring_read, 1)
                elif kind == "mx":
                    _, n, k = e
                    qt, h, k0, w, _ = max_pieces(n)[k]
                    dve.tensor_reduce(pmax[:, n % 2, qt, h, k0 // CH:k0 // CH + 1], bank[:, 0:w], AX_X,
                                      ALU.max).then_inc(ring_read, 1)
                elif kind == "mred":
                    n = e[1]
                    dve.wait_ge(ring_read, ring_at[("mx", n, len(max_pieces(n)) - 1)] + 1)
                    if n >= 2:
                        dve.wait_ge(nm_ready, n - 1)
                    dve.tensor_reduce(rmax[:, n % 2, :], pmax[:, n % 2, :, :, :].rearrange("p t h k -> p (t h) k"), AX_X,
                                      ALU.max).then_inc(mx_reduced, 1)
                elif kind == "mT":
                    n = e[1]
                    if n >= 2:
                        dve.wait_ge(m_landed[(n - 2) % 4], 32 * ((n - 2) // 4 + 1))
                    dve.tensor_copy(m_row[:, n % 2, :], bank[0:8, 0:CH // 2].bitcast(BF16)).then_inc(ring_read, 1)
                elif kind == "ocopy":
                    n = e[1]
                    dve.wait_ge(pv_done, max(u for u, (m, _) in enumerate(units) if m == n) + 1)
                    if n >= 1:
                        dve.wait_ge(ring_full, ring_at[("oT", n - 1)] + 1)
                    if n == 0:
                        dve.wait_ge(bias_landed, 16)
                    dve.tensor_copy(o_sb[:, :], psum[6 + n % 2][:, :]).then_inc(o_copied, 1)
                elif kind == "oT":
                    n = e[1]
                    c, g = n // G, n % G
                    view = bank[:, :].rearrange("p (t h w) -> p t h w", t=TPC, h=4)
                    step(dve.tensor_scalar(rsum[:, :, :], view[:, :, :, DK], TINY, None, ALU.max))
                    step(dve.reciprocal(rinv[:, :, :], rsum[:, :, :]))
                    if g == 0 and c:
                        dve.wait_ge(ring_full, ring_at[("gT", c - 1, 1)] + 1)
                    dve.tensor_tensor(att_sb[:, :, 64 * g:64 * (g + 1)].rearrange("p t (h d) -> p t h d", h=4),
                                      view[:, :, :, 0:DK], rinv[:, :, :].unsqueeze(3).to_broadcast([P, TPC, 4, DK]),
                                      ALU.mult).then_inc(ring_read, 1)
                elif kind == "gT":
                    _, c, half = e
                    if c:
                        dve.wait_ge(ring_full, ring_at[("wo", c - 1, 1)] + 1)
                    dst = att_t[:, :, :].rearrange("p a (t q) -> p t a q", q=P)[:, 2 * half:2 * half + 2, :, :]
                    dve.tensor_copy(dst, bank[:, :].rearrange("p (t a q) -> p t a q", t=2, a=KD)).then_inc(ring_read, 1)
                elif kind == "wo":
                    _, c, half = e
                    t0 = TPC * c + 2 * half
                    view = x_sb[:, t0:t0 + 2, :]
                    dve.tensor_tensor(view, bank[:, :].rearrange("p (t d) -> p t d", t=2), view,
                                      ALU.add).then_inc(ring_read, 1)
                elif kind == "logits":
                    c = e[1]
                    view = bank[:, 0:TPC * E].rearrange("p (t e) -> p t e", t=TPC)
                    step(dve.tensor_reduce(r_max[:, :], view, AX_X, ALU.max))
                    dve.tensor_tensor(r_log[:, :, :], view, r_max[:, :].unsqueeze(2).to_broadcast([P, TPC, E]),
                                      ALU.subtract).then_inc(r_log_ready, 1)
                    dve.wait_ge(r_log_ready, c + 1)
                    dve.memset(r_sum[:, :], 0.0).then_inc(ring_read, 1)
                elif kind == "rank":
                    c = e[1]
                    four = [P, TPC, E, E]
                    dve.wait_ge(r_exp_ready, c + 1)
                    dve.wait_ge(ring_read, ring_at[("logits", c)] + 1)
                    step(dve.tensor_reduce(r_sum[:, :], r_exp[:, :, :], AX_X, ALU.add))
                    step(dve.reciprocal(r_inv[:, :], r_sum[:, :]))
                    step(dve.tensor_tensor(r_prob[:, :, :], r_exp[:, :, :],
                                           r_inv[:, :].unsqueeze(2).to_broadcast([P, TPC, E]), ALU.mult))
                    other = r_prob[:, :, :].unsqueeze(2).to_broadcast(four)
                    own = r_prob[:, :, :].unsqueeze(3).to_broadcast(four)
                    dve.tensor_tensor(r_gt[:, :, :, :], other, own, ALU.is_gt).then_inc(dve_step, 1)
                    dve.tensor_tensor(r_eq[:, :, :, :], other, own, ALU.is_equal).then_inc(dve_step, 1)
                    steps[0] += 2
                    dve.wait_ge(dve_step, steps[0])
                    dve.wait_ge(consts, 8)
                    step(dve.tensor_tensor(r_eq[:, :, :, :], r_eq[:, :, :, :],
                                           lower[:, :, :].unsqueeze(1).to_broadcast(four), ALU.mult))
                    step(dve.tensor_tensor(r_gt[:, :, :, :], r_gt[:, :, :, :], r_eq[:, :, :, :], ALU.add))
                    step(dve.tensor_reduce(r_rank[:, :, :], r_gt[:, :, :, :], AX_X, ALU.add))
                    if c:
                        dve.wait_ge(ring_full, ring_at[("sT", c - 1)] + 1)
                    dve.scalar_tensor_tensor(out=scale_sb[:, :, :], in0=r_rank[:, :, :], scalar=1.5,
                                             in1=r_prob[:, :, :], op0=ALU.is_lt, op1=ALU.mult).then_inc(scale_ready, 1)
                elif kind == "sT":
                    c = e[1]
                    if c:
                        dve.wait_ge(s_stored[c - 1], 16)
                    dve.tensor_copy(sT_sb[:, :], bank[0:E, :]).then_inc(ring_read, 1)
                elif kind == "a":
                    _, c, ex = e
                    i = c * E + ex
                    if ex == 0:
                        dve.wait_ge(s_landed[c], 16)
                    if i == 0:
                        dve.wait_ge(st_full, last_st[3] + 1)
                    if i >= 2:
                        dve.wait_ge(silu_done, i - 1)
                    dve.tensor_tensor(u_sb[i % 2], bank[:, :], scale_bc[c % 2][:, ex, :], ALU.mult).then_inc(ring_read, 1)
                elif kind == "b":
                    _, c, ex = e
                    i = c * E + ex
                    if i >= 2:
                        dve.wait_ge(h_ready, i - 1)
                    dve.tensor_tensor(v_sb[i % 2], bank[:, :], scale_bc[c % 2][:, ex, :], ALU.mult).then_inc(ring_read, 1)
                elif kind == "h":
                    _, c, ex = e
                    i = c * E + ex
                    dve.wait_ge(silu_done, i + 1)
                    dve.wait_ge(ring_read, ring_at[("b", c, ex)] + 1)
                    if i >= 2:
                        dve.wait_ge(y_full, i - 1)
                    dve.tensor_tensor(h_sb[i % 2], g_sb[i % 2], v_sb[i % 2], ALU.mult).then_inc(h_ready, 1)
                elif kind == "out":
                    c = e[1]
                    dve.wait_ge(y_full, E * (c + 1))
                    for t in range(TPC):
                        view = x_sb[:, TPC * c + t, :]
                        last = dve.tensor_tensor(view, psum[Y_BANKS[t]][:, 0:D], view, ALU.add)
                    last.then_inc(y_added, 1)

        @block.tensor
        def _(pe):
            def make(e):
                i = ring_at[e]
                if i >= RING:
                    pe.wait_ge(ring_read, i - RING + 1)
                return ring_bank(e)

            def contract(dst, lhs, rhs):
                for a in range(KD):
                    last = pe.matmul(dst, lhs(a), rhs(a), start=(a == 0), stop=(a == KD - 1))
                return last

            for e in plan:
                kind = e[0]
                if kind == "kq":
                    _, what, m, c = e
                    w = min(CH, KEYS - CH * c) if what == "k" else CH
                    if what == "k":
                        if c == 0:
                            pe.wait_ge(ld["wk"], 16)
                        pe.wait_ge(ld_ctx[c], 16)
                        wt, moving = wk_sb, ctx_sb[:, :, CH * c:CH * c + w]
                    else:
                        if c == 0:
                            pe.wait_ge(ld["wq"], 16)
                        pe.wait_ge(ring_read, ring_at[("xT", 0, c, 1)] + 1)
                        wt, moving = wq_sb, xn_t[:, c % 2, :, :]
                    bank = make(e)
                    contract(bank[:, 0:w], lambda a: wt[:, a, P * m:P * (m + 1)],
                             lambda a: moving[:, a, :]).then_inc(ring_full, 1)
                elif kind == "v":
                    t = e[1]
                    r = key_rows(t)
                    if t == 0:
                        pe.wait_ge(ld["wv"], 16)
                    bank = make(e)
                    contract(bank[0:r, 0:D], lambda a: ctx_sb[:, a, P * t:P * t + r],
                             lambda a: wv_sb[:, a, :]).then_inc(ring_full, 1)
                elif kind == "xT":
                    _, second, c, half = e
                    if not second and c == 0:
                        pe.wait_ge(consts, 8)
                    pe.wait_ge(xn_ready, NC * second + c + 1)
                    bank = make(e)
                    for t in range(2):
                        for a in range(KD):
                            last = pe.transpose(bank[:, P * (2 * t + a):P * (2 * t + a + 1)],
                                                xn_sb[:, 2 * half + t, P * a:P * (a + 1)], ident[:, :])
                    last.then_inc(ring_full, 1)
                elif kind == "gate":
                    _, c, half = e
                    if (c, half) == (0, 0):
                        pe.wait_ge(ld["wg"], 16)
                    bank = make(e)
                    for t in range(2):
                        tile = P * (2 * half + t)
                        last = contract(bank[:, D * t:D * (t + 1)], lambda a: xn_t[:, c % 2, a, tile:tile + P],
                                        lambda a: wg_sb[:, a, :])
                    last.then_inc(ring_full, 1)
                elif kind == "mx":
                    _, n, k = e
                    c, g = n // G, n % G
                    qt, h, k0, w, diagonal = max_pieces(n)[k]
                    if k == 0:
                        if g == 0:
                            pe.wait_ge(q_landed[c], 16 * len(Q_PARTS))
                            pe.wait_ge(k_landed[c], 16 * len(K_PARTS))
                        if n == 0:
                            pe.wait_ge(bias_landed, 16)
                            pe.wait_ge(aug_rows, 2)
                    bank = make(e)
                    last = pe.matmul(bank[:, 0:w], qaug[0:ROW_MAX, c % 2, 4 * g + h, P * qt:P * (qt + 1)],
                                     kaug[0:ROW_MAX, 4 * g + h, k0:k0 + w], start=True, stop=not diagonal)
                    if diagonal:
                        d = P * ((w - 1) // P)
                        last = pe.matmul(bank[:, d:w], ident_b[:, :], tri_qk[:, 0:w - d], start=False, stop=True)
                    last.then_inc(ring_full, 1)
                elif kind == "mT":
                    n = e[1]
                    pe.wait_ge(nm_ready, n + 1)
                    bank = make(e)[0:8, 0:CH // 2].bitcast(BF16)
                    for t in range(TPC):
                        last = pe.transpose(bank[:, P * t:P * (t + 1)],
                                            nmax_b[:, n % 2, t, :, :].rearrange("p a h -> p (a h)"), ident_b[:, :])
                    last.then_inc(ring_full, 1)
                elif kind == "st":
                    _, u, n, j, h = e
                    c, g = n // G, n % G
                    i = st_at[(u, h)]
                    off = max(0, P * (j - TPC * c))
                    r = key_rows(j)
                    diagonal = j >= TPC * c
                    if j == 0 and h == 0:
                        pe.wait_ge(m_landed[n % 4], 32 * (n // 4 + 1))
                    if i >= ST_BANKS:
                        pe.wait_ge(exp_done, i - ST_BANKS + 1)
                    bank = psum[i % ST_BANKS]
                    last = pe.matmul(bank[0:r, off:CH], kaug[0:ROWS, 4 * g + h, P * j:P * j + r],
                                     qaug[0:ROWS, c % 2, 4 * g + h, off:CH], start=True, stop=not diagonal)
                    if diagonal:
                        last = pe.matmul(bank[0:r, off:off + P], ident_b[:, 0:r], tri_kq[:, :], start=False, stop=True)
                    last.then_inc(st_full, 1)
                elif kind == "pv":
                    _, u, n, j = e
                    c, g = n // G, n % G
                    off = max(0, P * (j - TPC * c))
                    r = key_rows(j)
                    if j == 0 and n >= 2:
                        pe.wait_ge(o_copied, n - 1)
                    pe.wait_ge(exp_done, st_at[(u, 3)] + 1)
                    for h in range(4):
                        col = (j * H + 4 * g + h) * VW
                        last = pe.matmul(psum[6 + n % 2][32 * h:32 * h + 32, off:CH], vaug[0:r, col:col + 32],
                                         probs[0:r, u % NSLOT, h, off:CH], start=(j == 0), stop=(j == key_tiles(c) - 1))
                    last.then_inc(pv_done, 1)
                elif kind == "oT":
                    n = e[1]
                    pe.wait_ge(o_copied, n + 1)
                    bank = make(e)
                    for t in range(TPC):
                        last = pe.transpose(bank[:, P * t:P * (t + 1)], o_sb[:, P * t:P * (t + 1)], ident[:, :])
                    last.then_inc(ring_full, 1)
                elif kind == "gT":
                    _, c, half = e
                    pe.wait_ge(gated, G * (c + 1))
                    bank = make(e)
                    for t in range(2):
                        for a in range(KD):
                            last = pe.transpose(bank[:, P * (2 * t + a):P * (2 * t + a + 1)],
                                                att_sb[:, 2 * half + t, P * a:P * (a + 1)], ident[:, :])
                    last.then_inc(ring_full, 1)
                elif kind == "wo":
                    _, c, half = e
                    if (c, half) == (0, 0):
                        pe.wait_ge(ld["wo"], 16)
                    pe.wait_ge(ring_read, ring_at[("gT", c, half)] + 1)
                    bank = make(e)
                    for t in range(2):
                        tile = P * (2 * half + t)
                        last = contract(bank[:, D * t:D * (t + 1)], lambda a: att_t[:, a, tile:tile + P],
                                        lambda a: wo_sb[:, a, :])
                    last.then_inc(ring_full, 1)
                elif kind == "logits":
                    c = e[1]
                    if c == 0:
                        pe.wait_ge(ld["gw"], 16)
                    pe.wait_ge(ring_read, ring_at[("xT", 1, c, 1)] + 1)
                    bank = make(e)
                    for t in range(TPC):
                        tile = P * t
                        last = contract(bank[:, E * t:E * (t + 1)], lambda a: gate_sb[:, c, CH * a + tile:CH * a + tile + P],
                                        lambda a: gw_sb[:, a, :])
                    last.then_inc(ring_full, 1)
                elif kind == "sT":
                    c = e[1]
                    pe.wait_ge(scale_ready, c + 1)
                    bank = make(e)
                    for t in range(TPC):
                        last = pe.transpose(bank[0:E, P * t:P * (t + 1)], scale_sb[:, t, :], ident[:, :])
                    last.then_inc(ring_full, 1)
                elif kind in ("a", "b"):
                    _, c, ex = e
                    if (c, ex) == (0, 0):
                        pe.wait_ge(ld["w1" if kind == "a" else "w3"], 16)
                    if ex == 0:
                        pe.wait_ge(ring_read, ring_at[("xT", 1, c, 1)] + 1)
                    wt = w1_sb if kind == "a" else w3_sb
                    bank = make(e)
                    contract(bank[:, :], lambda a: wt[:, ex, a, :],
                             lambda a: gate_sb[:, c, CH * a:CH * (a + 1)]).then_inc(ring_full, 1)
                elif kind == "y":
                    _, c, ex = e
                    i = c * E + ex
                    if i == 0:
                        pe.wait_ge(ld["w2"], 16)
                        pe.wait_ge(exp_done, len(st_at))
                        pe.wait_ge(o_copied, NC * G)
                    if ex == 0 and c:
                        pe.wait_ge(y_added, c)
                    pe.wait_ge(h_ready, i + 1)
                    for t in range(TPC):
                        last = pe.matmul(psum[Y_BANKS[t]][:, 0:D], h_sb[i % 2][:, P * t:P * (t + 1)], w2_sb[:, ex, :],
                                         start=(ex == 0), stop=(ex == E - 1))
                    last.then_inc(y_full, 1)


def kernel(x, ctx_1024, mask_BxS2_ik0, L0_xattn_Wq, L0_xattn_Wk, L0_xattn_Wv, L0_xattn_Wo, L0_xattn_Wg, L0_xattn_bg,
           L0_ffn_gate_w, L0_ffn_w1, L0_ffn_w2, L0_ffn_w3):
    import concourse.bacc as bacc
    from concourse.bass_utils import run_bass_kernel_spmd

    x, ctx_1024 = np.asarray(x), np.asarray(ctx_1024)
    arrays = {
        "x": x.reshape(TOK, D),
        "ctx_t": ctx_1024.reshape(KEYS, D).T,
        "mask": np.asarray(mask_BxS2_ik0).reshape(1, KEYS),
        "wq_t": np.asarray(L0_xattn_Wq).T,
        "wk_t": np.asarray(L0_xattn_Wk).T,
        "wv_t": np.asarray(L0_xattn_Wv).T,
        "wo_t": np.asarray(L0_xattn_Wo).T,
        "wg_t": np.asarray(L0_xattn_Wg).T,
        "bg": np.asarray(L0_xattn_bg),
        "gate_w": np.asarray(L0_ffn_gate_w),
        "w1": np.asarray(L0_ffn_w1),
        "w2": np.asarray(L0_ffn_w2),
        "w3": np.asarray(L0_ffn_w3),
    }
    arrays = {f"in_{k}": np.ascontiguousarray(a) for k, a in arrays.items()}
    nc = bacc.Bacc("TRN2", target_bir_lowering=False, num_devices=1)
    args = [nc.dram_tensor(k, a.shape, mybir.dt.from_np(a.dtype), kind="ExternalInput").ap() for k, a in arrays.items()]
    out = nc.dram_tensor("out", (TOK, D), F32, kind="ExternalOutput").ap()
    build(nc, *args, out)
    r = run_bass_kernel_spmd(nc, [arrays], core_ids=[0])
    return r.results[0]["out"].reshape(1, TOK, D)
```

```python
from contextlib import ExitStack

import numpy as np

import concourse.bass as bass
from concourse import mybir

F32 = mybir.dt.float32
BF16 = mybir.dt.bfloat16
F32R = mybir.dt.float32r
I32 = mybir.dt.int32
ALU = mybir.AluOpType
ACT = mybir.ActivationFunctionType
AX_X = mybir.AxisListType.X

P = 128
TOK, KEYS, D, H, DK = 2048, 1601, 256, 16, 16
E, HID = 8, 128
CH = 512
NC = TOK // CH
TPC = CH // P
NT = TOK // P
KT = (KEYS + P - 1) // P
KD = D // P
KP = 1602
G = H // 4
RING, RING0 = 4, 3
MAX_WIDTH = CH
ST_BANKS = 3
O_BANK = 7
NSLOT = 2
MASKED = -1.0e30
FLOOR = -1.0e20
TINY = 1.0e-30
MAX_PACE = 1.05
MAX_MARGIN = 40
EPS = 1e-5
VW = DK + 1
Y_BANKS = (0, 1, 2, 7)
Q_PARTS = (0, 0, 0, 1, 1, 2)
K_PARTS = (0, 1, 2, 0, 1, 0)
ROW_MASK = len(Q_PARTS) * DK
ROW_MAX = ROW_MASK + 1
ROWS = ROW_MAX + 2


TWO_ONES = float(np.uint32(0x3F803F80).view(np.float32))


def key_tiles(c):
    return min(TPC * (c + 1), KT)


def key_rows(j):
    return min(P, KEYS - P * j)


def max_pieces(n):
    c, out = n // G, []
    for h in range(4):
        for qt in range(TPC):
            i = TPC * c + qt
            seen = min(P * (i + 1), KEYS)
            pieces = -(-seen // MAX_WIDTH)
            width = P * -(-(-(-seen // P)) // pieces)
            for slot in range(pieces):
                k0 = slot * width
                w = min(width, seen - k0)
                out.append((qt, h, k0, w, i < KT and k0 + w == seen, slot))
    return out


def max_schedule():
    tiles = [sum((CH - max(0, P * (j - TPC * (n // G)))) // P for j in range(key_tiles(n // G))) * 4 for n in range(NC * G)]
    starts = [sum(tiles[:n]) for n in range(NC * G)]
    events, end = [], float("inf")
    for n in reversed(range(NC * G)):
        end = min(end, starts[n] - MAX_MARGIN)
        pieces = max_pieces(n)
        total = sum(w / P for _, _, _, w, _, _ in pieces)
        first = end - total / MAX_PACE
        done = 0
        for k, (_, _, _, w, _, _) in enumerate(pieces):
            events.append((first + done / MAX_PACE, n, 0, ("mx", n, k)))
            done += w / P
        events.append((end + 4, n, 1, ("mred", n)))
        events.append((end + 20, n, 2, ("mT", n)))
        end = first
    events.sort()
    return [(at, e) for at, _, _, e in events]


def make_plan():
    plan, due = [], []

    def later(unit, *events):
        due.extend((unit, e) for e in events)

    def emit_due(unit):
        now = [e for u, e in due if u <= unit]
        due[:] = [(u, e) for u, e in due if u > unit]
        plan.extend(now)

    maxes = max_schedule()
    spread = []
    for c in range(NC):
        part = plan if c < 2 else spread
        part.extend([("kq", "k", 0, c), ("stat", 0, c), ("kq", "k", 1, c), ("kload", c), ("norm", 0, c)])
        if c:
            part.extend([("v", t) for t in range(4 * c, min(4 * c + 2, KT))])
        part.extend([("xT0", c, 0), ("xT0", c, 1), ("kq", "q", 0, c), ("kq", "q", 1, c)])
        if c < 2:
            part.append(("qload", c))
        if c:
            part.extend([("v", t) for t in range(4 * c + 2, min(4 * c + 4, KT))])
        else:
            part.extend([("v", t) for t in range(4)])
        (spread if c else plan).extend([("gate", c, 0), ("gate", c, 1)])
    spread.append(("prologue_end",))
    early = [e for at, e in maxes if at < 0]
    maxes = [(at, e) for at, e in maxes if at >= 0]
    for i, e in enumerate(spread):
        plan.append(e)
        plan.extend(early[len(early) * i // len(spread):len(early) * (i + 1) // len(spread)])
    plan.append(("sigmoid",))

    units = [(n, j) for n in range(NC * G) for j in range(key_tiles(n // G))]
    position = 0

    def after_chunk(c, u):
        later(u + 4, ("gT", c, 0), ("gT", c, 1))
        later(u + 5, ("wo", c, 0), ("wo", c, 1), ("stat", 1, c))
        later(u + 6, ("norm", 1, c))
        later(u + 7, ("xT1", c, 0), ("xT1", c, 1))
        later(u + 8, ("logits", c), ("rexp", c))
        later(u + 9, ("rank", c))
        later(u + 10, ("sT", c))
        if c == 0:
            later(u + 11, ("xs", 0))

    for u, (n, j) in enumerate(units):
        for h in range(4):
            while maxes and maxes[0][0] <= position:
                plan.append(maxes.pop(0)[1])
            plan.append(("st", u, n, j, h))
            position += (CH - max(0, P * (j - TPC * (n // G)))) // P
        if u > 0:
            plan.append(("pv", u - 1, *units[u - 1]))
        emit_due(u)
        if u > 0 and units[u - 1][0] != n:
            m = n - 1
            plan.append(("ocopy", m))
            later(u + 1, ("oT", m))
            if m % G == G - 1:
                after_chunk(m // G, u)
                if m // G + 2 < NC:
                    plan.append(("qload", m // G + 2))
                if m // G == 2:
                    later(u + 1, ("sload", 0))
    u = len(units)
    plan.append(("pv", u - 1, *units[u - 1]))
    later(u, ("ocopy", NC * G - 1), ("oT", NC * G - 1))
    after_chunk(NC - 1, u - 3)
    todo = [(c, e) for c in range(NC) for e in range(E)]
    plan.append(("ws", 0))
    for i, (c, e) in enumerate(todo):
        if i == 1:
            later(u, ("sload", 1))
        if c == 0 and e + 1 < E:
            plan.append(("ws", e + 1))
        if i:
            plan.append(("hl", *todo[i - 1]))
        plan.append(("a", c, e))
        plan.extend([("b", c, e), ("h", c, e)])
        if e == 5 and c + 1 < NC:
            plan.append(("xs", c + 1))
        emit_due(u)
        u += 1
        if i:
            plan.append(("y", *todo[i - 1]))
            if e == 0:
                plan.append(("out", c - 1))
                if c + 1 < NC:
                    plan.append(("sload", c + 1))
    plan.extend([("hl", *todo[-1]), ("y", *todo[-1]), ("out", NC - 1)])
    return plan, units


RING_ITEMS = ("kq", "xT1", "gate", "mx", "mT", "oT", "gT", "wo", "logits", "sT", "a", "b")


def ring_places(items):
    places, owner, at = {}, [0] * RING, 0
    for i, e in enumerate(items):
        banks = 2 if e[0] == "mx" and max_pieces(e[1])[e[2]][3] > CH else 1
        if banks == 2:
            at += at % 2
        mine = [(at + k) % RING for k in range(banks)]
        places[e] = (mine[0], max(owner[k] for k in mine))
        for k in mine:
            owner[k] = i + 1
        at += banks
    return places


SIDE_ITEMS = ("v", "xT0")


def build(nc, x, ctx_t, mask, wq_t, wk_t, wv_t, wo_t, wg_t, bg, gate_w, w1, w2, w3, out):
    plan, units = make_plan()
    ring_at = {e: i for i, e in enumerate([e for e in plan if e[0] in RING_ITEMS])}
    places = ring_places(list(ring_at))
    side_at = {e: i for i, e in enumerate([e for e in plan if e[0] in SIDE_ITEMS])}
    kq_at = {e: i for i, e in enumerate([e for e in plan if e[0] == "kq"])}
    st_at = {(e[1], e[4]): i for i, e in enumerate([e for e in plan if e[0] == "st"])}
    last_st = {}
    for u, (n, _) in enumerate(units):
        last_st[n // G] = st_at[(u, 3)]
    prologue_items = max(i for e, i in ring_at.items() if e[0] in ("kq", "gate")) + 1

    with ExitStack() as ctx:
        def sb(name, shape, dt, stack=ctx):
            return stack.enter_context(nc.sbuf_tensor(name, shape, dt))

        def sem(name):
            return ctx.enter_context(nc.semaphore(name))

        def scratch(name, shape, dt):
            return nc.dram_tensor(name, shape, dt, kind="Internal").ap()

        k_parts = scratch("k_parts", (3, D, KEYS), BF16)
        q_parts = scratch("q_parts", (3, D, TOK), BF16)
        s_dram = scratch("s_dram", (E, TOK), F32)

        x_sb = sb("x_sb", [P, NT, D], F32)
        gate_sb = sb("gate_sb", [P, NC, TPC * D], F32)
        qaug = sb("qaug", [P, 2, H, CH], BF16)
        vaug = sb("vaug", [P, KT * H * VW + 16], F32)
        with ExitStack() as attention:
            kaug = sb("kaug", [P, H, KP], BF16, attention)
            probs = sb("probs", [P, NSLOT, 4, CH], F32, attention)
        w_hi = sb("w_hi", [P, E, 3, D], F32R)
        w_lo = sb("w_lo", [P, E, 3, D], F32R)
        h_hi = sb("h_hi", [P, 2, CH], F32R)
        h_lo = sb("h_lo", [P, 2, CH], F32R)
        u_sb = sb("u_sb", [P, 2, CH], F32)
        v_sb = sb("v_sb", [P, 2, CH], F32)
        x_lo1 = sb("x_lo1", [P, KD, CH], F32R)
        o_sb = sb("o_sb", [P, CH], F32)
        att_sb = sb("att_sb", [P, TPC, D], F32)
        att_t = sb("att_t", [P, KD, CH], F32)
        xn_sb = sb("xn_sb", [P, TPC, D], F32)
        wo_sb = sb("wo_sb", [P, KD, D], F32)
        gw_sb = sb("gw_sb", [P, KD, E], F32)
        ident = sb("ident", [P, P], F32)
        ident_b = sb("ident_b", [P, P], BF16)
        zero_b = sb("zero_b", [P, P], BF16)
        tri_qk = sb("tri_qk", [P, P], BF16)
        lower = sb("lower", [P, E, E], F32)
        ones_f = sb("ones_f", [P, E, E], F32)
        pmax = sb("pmax", [P, 2, TPC, 4, 4], F32)
        rmax = sb("rmax", [P, 2, TPC * 4], F32)
        nmax = sb("nmax", [P, 2, TPC * 4], F32)
        nmax_b = sb("nmax_b", [P, 2, TPC, 2, 4], BF16)
        m_row = sb("m_row", [8, 2, CH], BF16)
        stat6 = sb("stat6", [P, TPC, 6], F32)
        stat2 = sb("stat2", [P, TPC, 2], F32)
        var_e = sb("var_e", [P, TPC], F32)
        rstd = sb("rstd", [P, TPC], F32)
        minus_half = sb("minus_half", [P, TPC], F32)
        rsum = sb("rsum", [P, TPC, 4], F32)
        rinv = sb("rinv", [P, TPC, 4], F32)
        r_max = sb("r_max", [P, TPC], F32)
        r_log = sb("r_log", [P, TPC, E], F32)
        r_exp = sb("r_exp", [P, TPC, E], F32)
        r_sum = sb("r_sum", [P, TPC], F32)
        r_inv = sb("r_inv", [P, TPC], F32)
        r_prob = sb("r_prob", [P, TPC, E], F32)
        r_gt, r_eq = (att_t[:, a, 0:TPC * E * E].rearrange("p (t i j) -> p t i j", t=TPC, i=E) for a in (0, 1))
        r_rank = sb("r_rank", [P, TPC, E], F32)
        scale_sb = sb("scale_sb", [P, TPC, E], F32)
        sT_sb = sb("sT_sb", [E, CH], F32)
        with ExitStack() as early:
            ctx_sb = sb("ctx_sb", [P, KD, KEYS], F32, early)
            wq_sb = sb("wq_sb", [P, KD, D], F32, early)
            wk_sb = sb("wk_sb", [P, KD, D], F32, early)
            wv_sb = sb("wv_sb", [P, KD, D], F32, early)
            wg_sb = sb("wg_sb", [P, KD, D], F32, early)
            xn_t = sb("xn_t", [P, 2, KD, CH], F32, early)
            bg_sb = sb("bg_sb", [P, D], F32, early)
            mask_i = sb("mask_i", [1, KEYS], I32, early)
        w_sb = sb("w_sb", [P, E, 3, D], F32)
        x_hi = sb("x_hi", [P, 2, KD, CH], F32R)
        x_lo0 = sb("x_lo0", [P, KD, CH], F32R)
        x_lo = (x_lo0, x_lo1)
        stage_words = probs[:, :, :, :].rearrange("p s h q -> p (s h q)")
        stage = [stage_words[:, 768 * s:768 * (s + 1)].bitcast(BF16).rearrange("p (a q) -> p a q", a=3) for s in range(2)]
        rest = [stage_words[:, 2048 + CH * s:2048 + CH * (s + 1)] for s in range(2)]
        scale_bc = [qaug[:, s, :, :].rearrange("p h q -> p (h q)").bitcast(F32).rearrange("p (e q) -> p e q", e=E)
                    for s in range(2)]
        vflat = vaug[:, 0:KT * H * VW].rearrange("p (t h w) -> p t h w", t=KT, h=H)
        ones_row = gate_sb[0:ROWS - ROW_MASK, NC - 1, :].bitcast(BF16)[:, 0:KP]
        bias_row = att_t[0:1, :, :].rearrange("p a q -> p (a q)").bitcast(BF16)[:, 0:KEYS]

        psum = {i: ctx.enter_context(nc.psum_tensor(f"bank{i}", [P, CH], F32)) for i in range(RING0)}
        ring = ctx.enter_context(nc.psum_tensor("ring", [P, RING * CH], F32))
        psum[O_BANK] = ctx.enter_context(nc.psum_tensor(f"bank{O_BANK}", [P, CH], F32))

        def side_bank(e):
            return psum[side_at[e] % ST_BANKS]

        def ring_bank(e):
            first = places[e][0]
            return ring[:, CH * first:CH * (first + (2 if e[0] == "mx" and first % 2 == 0 else 1))]

        ld = {k: sem(f"ld_{k}") for k in ("wk", "wq", "wv", "wg", "bg", "wo", "gw", "mask", "w1", "w3", "w2")}
        ld_ctx = [sem(f"ld_ctx{i}") for i in range(NC)]
        ld_x = [sem(f"ld_x{i}") for i in range(NC)]
        consts = sem("consts")
        aug_src = sem("aug_src")
        aug_k = sem("aug_k")
        aug_q = sem("aug_q")
        v_ones = sem("v_ones")
        bias_ready = sem("bias_ready")
        bias_landed = sem("bias_landed")
        ring_full = sem("ring_full")
        ring_read = sem("ring_read")
        hi_ready = sem("hi_ready")
        mid_ready = sem("mid_ready")
        lo_ready = sem("lo_ready")
        parts_out = [sem(f"parts_out{i}") for i in range(2)]
        k_landed = [sem(f"k_landed{i}") for i in range(NC)]
        q_landed = [sem(f"q_landed{i}") for i in range(NC)]
        var_ready = sem("var_ready")
        rstd_ready = sem("rstd_ready")
        side_full = sem("side_full")
        side_read = sem("side_read")
        xn_ready = sem("xn_ready")
        gate_ready = sem("gate_ready")
        st_full = sem("st_full")
        exp_done = sem("exp_done")
        pv_done = sem("pv_done")
        mx_reduced = sem("mx_reduced")
        nm_ready = sem("nm_ready")
        nm_step = sem("nm_step")
        m_landed = [sem(f"m_landed{i}") for i in range(4)]
        o_copied = sem("o_copied")
        gated = sem("gated")
        r_log_ready = sem("r_log_ready")
        r_exp_ready = sem("r_exp_ready")
        scale_ready = sem("scale_ready")
        s_stored = [sem(f"s_stored{i}") for i in range(NC)]
        s_landed = [sem(f"s_landed{i}") for i in range(NC)]
        w_hi_ready = sem("w_hi_ready")
        w_lo_ready = sem("w_lo_ready")
        x_hi_ready = sem("x_hi_ready")
        x_lo_ready = sem("x_lo_ready")
        silu_done = sem("silu_done")
        h_ready = sem("h_ready")
        h_hi_ready = sem("h_hi_ready")
        h_lo_ready = sem("h_lo_ready")
        y_full = sem("y_full")
        y_added = sem("y_added")
        out_done = sem("out_done")
        dve_step = sem("dve_step")
        block = ctx.enter_context(nc.Block())

        @block.sync
        def _(sp):
            def tiles(w):
                return w.rearrange("(a p) n -> p a n", p=P)

            sp.dma_start(wk_sb[:, :, :], tiles(wk_t)).then_inc(ld["wk"], 16)
            last_rows = ROWS - ROW_MASK
            for c in range(NC):
                k0, k1 = CH * c, min(CH * (c + 1), KEYS)
                sp.dma_start(ctx_sb[:, :, k0:k1], tiles(ctx_t)[:, :, k0:k1]).then_inc(ld_ctx[c], 16)
            for name, dst, src in (("wq", wq_sb, wq_t), ("wg", wg_sb, wg_t), ("wo", wo_sb, wo_t), ("gw", gw_sb, gate_w)):
                sp.dma_start(dst[:, :, :], tiles(src)).then_inc(ld[name], 16)
            sp.wait_ge(aug_src, 1)
            sp.dma_start(kaug[ROW_MASK:ROWS, :, :], ones_row.unsqueeze(1).to_broadcast([last_rows, H, KP])).then_inc(aug_k, 16)
            sp.dma_start(qaug[ROW_MASK:ROWS, :, :, :].rearrange("p s h q -> p (s h) q"),
                         ones_row[:, 0:CH].unsqueeze(1).to_broadcast([last_rows, 2 * H, CH])).then_inc(aug_q, 16)
            for e in plan:
                kind = e[0]
                if kind == "kq":
                    i, (_, what, m, c) = kq_at[e], e
                    w = min(CH, KEYS - CH * c) if what == "k" else CH
                    parts = k_parts if what == "k" else q_parts
                    sp.wait_ge(hi_ready, i + 1)
                    sp.wait_ge(mid_ready, i + 1)
                    sp.wait_ge(lo_ready, i + 1)
                    sp.dma_start(parts[:, P * m:P * (m + 1), CH * c:CH * c + w].rearrange("a p q -> p a q"),
                                 stage[i % 2][:, :, 0:w]).then_inc(parts_out[i % 2], 16)
                elif kind in ("kload", "qload"):
                    c, what = e[1], kind[0]
                    i = kq_at[("kq", what, 1, c)]
                    sp.wait_ge(parts_out[i % 2], 16 * (i // 2 + 1))
                    sp.wait_ge(parts_out[(i - 1) % 2], 16 * ((i - 1) // 2 + 1))
                    if what == "q" and c >= 2:
                        sp.wait_ge(st_full, last_st[c - 2] + 1)
                    w = min(CH, KEYS - CH * c) if what == "k" else CH
                    for r in range(len(Q_PARTS)):
                        if what == "k":
                            dst = kaug[DK * r:DK * (r + 1), :, CH * c:CH * c + w]
                            src = k_parts[K_PARTS[r], :, CH * c:CH * c + w]
                        else:
                            dst = qaug[DK * r:DK * (r + 1), c % 2, :, :]
                            src = q_parts[Q_PARTS[r], :, CH * c:CH * c + w]
                        sp.dma_start(dst, src.rearrange("(h d) q -> d h q", d=DK)
                                     ).then_inc((k_landed if what == "k" else q_landed)[c], 16)
                    if what == "k" and c == 0:
                        sp.wait_ge(aug_k, 16)
                        sp.wait_ge(bias_ready, 1)
                        sp.dma_start(kaug[ROW_MASK:ROW_MASK + 1, :, 0:KEYS],
                                     bias_row.unsqueeze(1).to_broadcast([1, H, KEYS])).then_inc(bias_landed, 16)
                elif kind == "mT":
                    n = e[1]
                    c, g = n // G, n % G
                    sp.wait_ge(ring_read, ring_at[e] + 1)
                    sp.wait_ge(aug_q, 16)
                    for part in range(2):
                        sp.dma_start(qaug[ROW_MAX + part:ROW_MAX + part + 1, c % 2, 4 * g:4 * g + 4, :],
                                     m_row[4 * part:4 * part + 4, n % 2, :]).then_inc(m_landed[n % 4], 16)
                elif kind == "prologue_end":
                    sp.wait_ge(ring_full, prologue_items)
                    sp.wait_ge(ring_read, prologue_items)
                    sp.wait_ge(side_read, len(side_at))
                    for part, name, src in ((0, "w1", w1), (1, "w3", w3)):
                        dst = w_sb[:, :, part, :].rearrange("p e (a h) -> p e a h", a=KD)
                        for a in range(KD):
                            sp.dma_start(dst[:, :, a, :], src[:, P * a:P * (a + 1), :].rearrange("e p h -> p e h")
                                         ).then_inc(ld[name], 16)
                    sp.dma_start(w_sb[:, :, 2, :], w2.rearrange("e h d -> h e d")).then_inc(ld["w2"], 16)
                elif kind == "sT":
                    c = e[1]
                    sp.wait_ge(ring_read, ring_at[e] + 1)
                    sp.dma_start(s_dram[:, CH * c:CH * (c + 1)], sT_sb[:, :]).then_inc(s_stored[c], 16)
                elif kind == "sload":
                    c = e[1]
                    sp.wait_ge(s_stored[c], 16)
                    if c == 0:
                        sp.wait_ge(st_full, last_st[2] + 1)
                    elif c == 1:
                        sp.wait_ge(st_full, last_st[3] + 1)
                    else:
                        sp.wait_ge(ring_read, ring_at[("b", c - 2, E - 1)] + 1)
                    sp.dma_start(scale_bc[c % 2], s_dram[:, CH * c:CH * (c + 1)].partition_broadcast(P)
                                 ).then_inc(s_landed[c], 16)
                elif kind == "out":
                    c = e[1]
                    sp.wait_ge(y_added, c + 1)
                    sp.dma_start(out.rearrange("(t p) d -> p t d", p=P)[:, TPC * c:TPC * (c + 1), :],
                                 x_sb[:, TPC * c:TPC * (c + 1), :]).then_inc(out_done, 16)
            sp.wait_ge(out_done, 16 * NC)

        @block.gpsimd
        def _(pool):
            def select(dst, src, pattern, base, mult, op, fill):
                return pool.affine_select(out=dst, in_=src, compare_op=op, fill=fill, base=base,
                                          pattern=pattern, channel_multiplier=mult)

            pool.memset(ones_row.bitcast(F32), TWO_ONES).then_inc(aug_src, 1)
            pool.memset(zero_b[:, :], 0.0).then_inc(consts, 1)
            pool.memset(ident[:, :], 0.0).then_inc(consts, 1)
            pool.memset(ones_f[:, :, :], 1.0).then_inc(consts, 1)
            pool.memset(minus_half[:, :], -0.5).then_inc(consts, 1)
            pool.wait_ge(consts, 4)
            select(ident[:, :], ident[:, :], [[-1, P]], 0, 1, ALU.not_equal, 1.0).then_inc(consts, 1)
            select(ident_b[:, :], zero_b[:, :], [[-1, P]], 0, 1, ALU.not_equal, 1.0).then_inc(consts, 1)
            select(tri_qk[:, :], zero_b[:, :], [[-1, P]], 0, 1, ALU.is_ge, MASKED).then_inc(consts, 1)
            select(lower[:, :, :], ones_f[:, :, :], [[1, E], [-1, E]], 0, 0, ALU.is_gt, 0.0).then_inc(consts, 1)
            norms = 0
            for e in plan:
                kind = e[0]
                if kind == "stat":
                    norms += 1
                    pool.wait_ge(var_ready, norms)
                    if norms > 1:
                        pool.wait_ge(xn_ready, norms - 1)
                    pool.tensor_tensor(rstd[:, :], var_e[:, :], minus_half[:, :], ALU.pow).then_inc(rstd_ready, 1)
                elif kind == "kq":
                    i, (_, what, m, c) = kq_at[e], e
                    w = min(CH, KEYS - CH * c) if what == "k" else CH
                    pool.wait_ge(ring_read, ring_at[e] + 1)
                    pool.wait_ge(mid_ready, i + 1)
                    pool.tensor_tensor(stage[i % 2][:, 2, 0:w], rest[i % 2][:, 0:w], stage[i % 2][:, 1, 0:w],
                                       ALU.subtract).then_inc(lo_ready, 1)
                elif kind == "mred":
                    n = e[1]
                    s = n % 2
                    view = nmax[:, s, :].rearrange("p (t h) -> p t h", t=TPC)
                    pool.wait_ge(mx_reduced, n + 1)
                    if n >= 2:
                        pool.wait_ge(ring_read, ring_at[("mT", n - 2)] + 1)
                    pool.tensor_scalar(nmax[:, s, :], rmax[:, s, :], FLOOR, -1.0, ALU.max, ALU.mult).then_inc(nm_step, 1)
                    pool.wait_ge(nm_step, 2 * n + 1)
                    pool.tensor_copy(nmax_b[:, s, :, 0, :], view).then_inc(nm_step, 1)
                    pool.wait_ge(nm_step, 2 * n + 2)
                    pool.tensor_tensor(nmax_b[:, s, :, 1, :], view, nmax_b[:, s, :, 0, :], ALU.subtract).then_inc(nm_ready, 1)
                elif kind == "oT":
                    n = e[1]
                    c, g = n // G, n % G
                    view = att_sb[:, :, 64 * g:64 * (g + 1)]
                    pool.wait_ge(ring_read, ring_at[e] + 1)
                    pool.wait_ge(gate_ready, c + 1)
                    pool.tensor_tensor(view, view,
                                       gate_sb[:, c, :].rearrange("p (t d) -> p t d", t=TPC)[:, :, 64 * g:64 * (g + 1)],
                                       ALU.mult).then_inc(gated, 1)

        @block.scalar
        def _(act):
            xv = x.rearrange("(t p) d -> p t d", p=P)
            act.dma_start(mask_i[:, :], mask).then_inc(ld["mask"], 16)
            act.dma_start(x_sb[:, 0:TPC, :], xv[:, 0:TPC, :]).then_inc(ld_x[0], 16)
            act.dma_start(wv_sb[:, :, :], wv_t.rearrange("(a p) n -> p a n", p=P)).then_inc(ld["wv"], 16)
            act.dma_start(bg_sb[:, :], bg.partition_broadcast(P)).then_inc(ld["bg"], 16)
            for c in range(1, NC):
                act.dma_start(x_sb[:, TPC * c:TPC * (c + 1), :], xv[:, TPC * c:TPC * (c + 1), :]).then_inc(ld_x[c], 16)
            for e in plan:
                kind = e[0]
                if kind == "kq":
                    i, (_, what, m, c) = kq_at[e], e
                    w = min(CH, KEYS - CH * c) if what == "k" else CH
                    act.wait_ge(ring_full, ring_at[e] + 1)
                    if i >= 2:
                        act.wait_ge(parts_out[i % 2], 16 * (i // 2))
                    act.activation(stage[i % 2][:, 0, 0:w], ring_bank(e)[:, 0:w], ACT.Copy).then_inc(hi_ready, 1)
                    act.wait_ge(ring_read, ring_at[e] + 1)
                    act.activation(stage[i % 2][:, 1, 0:w], rest[i % 2][:, 0:w], ACT.Copy).then_inc(mid_ready, 1)
                elif kind == "v":
                    t = e[1]
                    r = key_rows(t)
                    if t == 0:
                        act.wait_ge(v_ones, 2)
                    act.wait_ge(side_full, side_at[e] + 1)
                    act.activation(vflat[0:r, t, :, 0:DK], side_bank(e)[0:r, 0:D].rearrange("p (h d) -> p h d", h=H),
                                   ACT.Copy).then_inc(side_read, 1)
                elif kind == "xT0":
                    _, c, half = e
                    if c >= 2:
                        act.wait_ge(ring_full, ring_at[("gate", c - 2, 1)] + 1)
                    act.wait_ge(side_full, side_at[e] + 1)
                    dst = xn_t[:, c % 2, :, :].rearrange("p a (t q) -> p t a q", q=P)[:, 2 * half:2 * half + 2, :, :]
                    act.activation(dst, side_bank(e)[:, :].rearrange("p (t a q) -> p t a q", t=2, a=KD),
                                   ACT.Copy).then_inc(side_read, 1)
                elif kind == "sigmoid":
                    for c in range(NC):
                        act.wait_ge(ring_read, ring_at[("gate", c, 1)] + 1)
                        act.activation(gate_sb[:, c, :], gate_sb[:, c, :], ACT.Sigmoid).then_inc(gate_ready, 1)
                elif kind == "ocopy":
                    n = e[1]
                    act.wait_ge(pv_done, max(u for u, (m, _) in enumerate(units) if m == n) + 1)
                    if n >= 1:
                        act.wait_ge(ring_full, ring_at[("oT", n - 1)] + 1)
                    act.activation(o_sb[:, :], psum[O_BANK][:, :], ACT.Copy).then_inc(o_copied, 1)
                elif kind == "st":
                    _, u, n, j, h = e
                    i = st_at[(u, h)]
                    off = max(0, P * (j - TPC * (n // G)))
                    rows = key_rows(j)
                    if i == 0:
                        for s in range(2):
                            act.wait_ge(parts_out[s], 16 * (len(kq_at) // 2))
                    act.wait_ge(st_full, i + 1)
                    if u >= NSLOT:
                        act.wait_ge(pv_done, u - NSLOT + 1)
                    act.activation(probs[0:rows, u % NSLOT, h, off:CH], psum[i % ST_BANKS][0:rows, off:CH], ACT.Exp,
                                   scale=DK ** -0.5).then_inc(exp_done, 1)
                elif kind == "rexp":
                    c = e[1]
                    act.wait_ge(r_log_ready, c + 1)
                    act.activation(r_exp[:, :, :], r_log[:, :, :], ACT.Exp).then_inc(r_exp_ready, 1)
                elif kind == "ws":
                    ex = e[1]
                    if ex == 0:
                        for name, times in (("w1", KD), ("w3", KD), ("w2", 1)):
                            act.wait_ge(ld[name], 16 * times)
                        act.wait_ge(pv_done, len(units))
                    act.activation(w_hi[:, ex, :, :], w_sb[:, ex, :, :], ACT.Copy).then_inc(w_hi_ready, 1)
                elif kind == "xs":
                    c = e[1]
                    act.wait_ge(ring_read, ring_at[("xT1", c, 1)] + 1)
                    if c == 0:
                        act.wait_ge(ld["w2"], 16)
                    if c >= 2:
                        act.wait_ge(ring_full, ring_at[("b", c - 2, E - 1)] + 1)
                    act.activation(x_hi[:, c % 2, :, :], gate_sb[:, c, :].rearrange("p (a q) -> p a q", a=KD),
                                   ACT.Copy).then_inc(x_hi_ready, 1)
                elif kind == "h":
                    _, c, ex = e
                    i = c * E + ex
                    act.wait_ge(ring_read, ring_at[("a", c, ex)] + 1)
                    act.activation(u_sb[:, i % 2, :], u_sb[:, i % 2, :], ACT.Silu).then_inc(silu_done, 1)
                elif kind == "hl":
                    _, c, ex = e
                    i = c * E + ex
                    act.wait_ge(h_ready, i + 1)
                    if i >= 2:
                        act.wait_ge(y_full, i - 1)
                    act.activation(h_hi[:, i % 2, :], v_sb[:, i % 2, :], ACT.Copy).then_inc(h_hi_ready, 1)

        @block.vector
        def _(dve):
            steps = [0]

            def step(ins):
                ins.then_inc(dve_step, 1)
                steps[0] += 1
                dve.wait_ge(dve_step, steps[0])

            dve.memset(vaug[:, :], 1.0).then_inc(v_ones, 1)
            dve.memset(pmax[:, :, :, :, :], MASKED).then_inc(v_ones, 1)
            dve.wait_ge(ld["mask"], 16)
            dve.tensor_scalar(bias_row, mask_i[:, :], 0, MASKED, ALU.is_equal, ALU.mult).then_inc(bias_ready, 1)
            dve.wait_ge(v_ones, 2)
            norms = 0
            for e in plan:
                kind = e[0]
                if kind in RING_ITEMS:
                    dve.wait_ge(ring_full, ring_at[e] + 1)
                    bank = ring_bank(e)
                if kind == "kq":
                    i, (_, what, m, c) = kq_at[e], e
                    w = min(CH, KEYS - CH * c) if what == "k" else CH
                    dve.wait_ge(hi_ready, i + 1)
                    if i >= 2:
                        dve.wait_ge(lo_ready, i - 1)
                    dve.tensor_tensor(rest[i % 2][:, 0:w], bank[:, 0:w], stage[i % 2][:, 0, 0:w],
                                      ALU.subtract).then_inc(ring_read, 1)
                elif kind == "stat":
                    _, second, c = e
                    if not second:
                        dve.wait_ge(ld_x[c], 16)
                    else:
                        dve.wait_ge(ring_read, ring_at[("wo", c, 1)] + 1)
                    for t in range(TPC):
                        last = dve.bn_stats(stat6[:, t, :], x_sb[:, TPC * c + t, :])
                    step(last)
                    for t in range(TPC):
                        last = dve.bn_aggr(stat2[:, t, :], stat6[:, t, :])
                    step(last)
                    dve.tensor_scalar(var_e[:, :], stat2[:, :, 1], EPS, None, ALU.add).then_inc(var_ready, 1)
                elif kind == "norm":
                    _, second, c = e
                    norms += 1
                    dve.wait_ge(rstd_ready, norms)
                    if norms > 1:
                        if second and c:
                            dve.wait_ge(ring_full, ring_at[("xT1", c - 1, 1)] + 1)
                        else:
                            dve.wait_ge(side_full, side_at[("xT0", (c - 1) % NC, 1)] + 1)
                    for t in range(TPC):
                        last = dve.tensor_scalar(xn_sb[:, t, :], x_sb[:, TPC * c + t, :], stat2[:, t, 0:1],
                                                 rstd[:, t:t + 1], ALU.subtract, ALU.mult)
                    last.then_inc(xn_ready, 1)
                elif kind == "xT1":
                    _, c, half = e
                    dve.wait_ge(gated, G * (c + 1))
                    dst = gate_sb[:, c, :].rearrange("p (a q) -> p a q", a=KD)
                    dst = dst.rearrange("p a (t q) -> p t a q", q=P)[:, 2 * half:2 * half + 2, :, :]
                    dve.tensor_copy(dst, bank[:, :].rearrange("p (t a q) -> p t a q", t=2, a=KD)).then_inc(ring_read, 1)
                elif kind == "gate":
                    _, c, half = e
                    if (c, half) == (0, 0):
                        dve.wait_ge(ld["bg"], 16)
                    if (c, half) == (NC - 1, 0):
                        dve.wait_ge(aug_k, 16)
                        dve.wait_ge(aug_q, 16)
                    dve.tensor_tensor(gate_sb[:, c, CH * half:CH * (half + 1)].rearrange("p (t d) -> p t d", t=2),
                                      bank[:, :].rearrange("p (t d) -> p t d", t=2),
                                      bg_sb[:, :].unsqueeze(1).to_broadcast([P, 2, D]), ALU.add).then_inc(ring_read, 1)
                elif kind == "mx":
                    _, n, k = e
                    qt, h, k0, w, _, slot = max_pieces(n)[k]
                    dve.tensor_reduce(pmax[:, n % 2, qt, h, slot:slot + 1], bank[:, 0:w], AX_X,
                                      ALU.max).then_inc(ring_read, 1)
                elif kind == "mred":
                    n = e[1]
                    dve.wait_ge(ring_read, ring_at[("mx", n, len(max_pieces(n)) - 1)] + 1)
                    if n >= 2:
                        dve.wait_ge(nm_ready, n - 1)
                    dve.tensor_reduce(rmax[:, n % 2, :], pmax[:, n % 2, :, :, :].rearrange("p t h k -> p (t h) k"), AX_X,
                                      ALU.max).then_inc(mx_reduced, 1)
                elif kind == "mT":
                    n = e[1]
                    if n >= 2:
                        dve.wait_ge(m_landed[(n - 2) % 4], 32 * ((n - 2) // 4 + 1))
                    dve.tensor_copy(m_row[:, n % 2, :], bank[0:8, 0:CH // 2].bitcast(BF16)).then_inc(ring_read, 1)
                elif kind == "oT":
                    n = e[1]
                    c, g = n // G, n % G
                    view = bank[:, :].rearrange("p (t h w) -> p t h w", t=TPC, h=4)
                    if n == 0:
                        dve.wait_ge(bias_landed, 16)
                    step(dve.tensor_scalar(rsum[:, :, :], view[:, :, :, DK], TINY, None, ALU.max))
                    step(dve.reciprocal(rinv[:, :, :], rsum[:, :, :]))
                    if g == 0 and c:
                        dve.wait_ge(ring_full, ring_at[("gT", c - 1, 1)] + 1)
                    dve.tensor_tensor(att_sb[:, :, 64 * g:64 * (g + 1)].rearrange("p t (h d) -> p t h d", h=4),
                                      view[:, :, :, 0:DK], rinv[:, :, :].unsqueeze(3).to_broadcast([P, TPC, 4, DK]),
                                      ALU.mult).then_inc(ring_read, 1)
                elif kind == "gT":
                    _, c, half = e
                    if c:
                        dve.wait_ge(ring_full, ring_at[("wo", c - 1, 1)] + 1)
                    dst = att_t[:, :, :].rearrange("p a (t q) -> p t a q", q=P)[:, 2 * half:2 * half + 2, :, :]
                    dve.tensor_copy(dst, bank[:, :].rearrange("p (t a q) -> p t a q", t=2, a=KD)).then_inc(ring_read, 1)
                elif kind == "wo":
                    _, c, half = e
                    t0 = TPC * c + 2 * half
                    view = x_sb[:, t0:t0 + 2, :]
                    dve.tensor_tensor(view, bank[:, :].rearrange("p (t d) -> p t d", t=2), view,
                                      ALU.add).then_inc(ring_read, 1)
                elif kind == "logits":
                    c = e[1]
                    view = bank[:, 0:TPC * E].rearrange("p (t e) -> p t e", t=TPC)
                    step(dve.tensor_reduce(r_max[:, :], view, AX_X, ALU.max))
                    dve.tensor_tensor(r_log[:, :, :], view, r_max[:, :].unsqueeze(2).to_broadcast([P, TPC, E]),
                                      ALU.subtract).then_inc(r_log_ready, 1)
                    dve.wait_ge(r_log_ready, c + 1)
                    dve.memset(r_sum[:, :], 0.0).then_inc(ring_read, 1)
                elif kind == "rank":
                    c = e[1]
                    four = [P, TPC, E, E]
                    dve.wait_ge(r_exp_ready, c + 1)
                    dve.wait_ge(ring_read, ring_at[("logits", c)] + 1)
                    step(dve.tensor_reduce(r_sum[:, :], r_exp[:, :, :], AX_X, ALU.add))
                    step(dve.reciprocal(r_inv[:, :], r_sum[:, :]))
                    step(dve.tensor_tensor(r_prob[:, :, :], r_exp[:, :, :],
                                           r_inv[:, :].unsqueeze(2).to_broadcast([P, TPC, E]), ALU.mult))
                    other = r_prob[:, :, :].unsqueeze(2).to_broadcast(four)
                    own = r_prob[:, :, :].unsqueeze(3).to_broadcast(four)
                    dve.tensor_tensor(r_gt[:, :, :, :], other, own, ALU.is_gt).then_inc(dve_step, 1)
                    dve.tensor_tensor(r_eq[:, :, :, :], other, own, ALU.is_equal).then_inc(dve_step, 1)
                    steps[0] += 2
                    dve.wait_ge(dve_step, steps[0])
                    dve.wait_ge(consts, 8)
                    step(dve.tensor_tensor(r_eq[:, :, :, :], r_eq[:, :, :, :],
                                           lower[:, :, :].unsqueeze(1).to_broadcast(four), ALU.mult))
                    step(dve.tensor_tensor(r_gt[:, :, :, :], r_gt[:, :, :, :], r_eq[:, :, :, :], ALU.add))
                    step(dve.tensor_reduce(r_rank[:, :, :], r_gt[:, :, :, :], AX_X, ALU.add))
                    if c:
                        dve.wait_ge(ring_full, ring_at[("sT", c - 1)] + 1)
                    dve.scalar_tensor_tensor(out=scale_sb[:, :, :], in0=r_rank[:, :, :], scalar=1.5,
                                             in1=r_prob[:, :, :], op0=ALU.is_lt, op1=ALU.mult).then_inc(scale_ready, 1)
                elif kind == "sT":
                    c = e[1]
                    if c:
                        dve.wait_ge(s_stored[c - 1], 16)
                    dve.tensor_copy(sT_sb[:, :], bank[0:E, :]).then_inc(ring_read, 1)
                elif kind == "ws":
                    ex = e[1]
                    dve.wait_ge(w_hi_ready, ex + 1)
                    dve.tensor_tensor(w_lo[:, ex, :, :], w_sb[:, ex, :, :], w_hi[:, ex, :, :], ALU.subtract).then_inc(w_lo_ready, 1)
                elif kind == "xs":
                    c = e[1]
                    dve.wait_ge(x_hi_ready, c + 1)
                    dve.tensor_tensor(x_lo[c % 2][:, :, :], gate_sb[:, c, :].rearrange("p (a q) -> p a q", a=KD),
                                      x_hi[:, c % 2, :, :], ALU.subtract).then_inc(x_lo_ready, 1)
                elif kind == "a":
                    _, c, ex = e
                    i = c * E + ex
                    if ex == 0:
                        dve.wait_ge(s_landed[c], 16)
                    if i >= 2:
                        dve.wait_ge(h_ready, i - 1)
                    dve.tensor_tensor(u_sb[:, i % 2, :], bank[:, :], scale_bc[c % 2][:, ex, :], ALU.mult).then_inc(ring_read, 1)
                elif kind == "b":
                    _, c, ex = e
                    i = c * E + ex
                    if i >= 2:
                        dve.wait_ge(h_lo_ready, i - 1)
                    dve.tensor_tensor(v_sb[:, i % 2, :], bank[:, :], scale_bc[c % 2][:, ex, :], ALU.mult).then_inc(ring_read, 1)
                elif kind == "h":
                    _, c, ex = e
                    i = c * E + ex
                    dve.wait_ge(silu_done, i + 1)
                    dve.wait_ge(ring_read, ring_at[("b", c, ex)] + 1)
                    dve.tensor_tensor(v_sb[:, i % 2, :], u_sb[:, i % 2, :], v_sb[:, i % 2, :], ALU.mult).then_inc(h_ready, 1)
                elif kind == "hl":
                    _, c, ex = e
                    i = c * E + ex
                    dve.wait_ge(h_hi_ready, i + 1)
                    dve.tensor_tensor(h_lo[:, i % 2, :], v_sb[:, i % 2, :], h_hi[:, i % 2, :], ALU.subtract).then_inc(h_lo_ready, 1)
                elif kind == "out":
                    c = e[1]
                    dve.wait_ge(y_full, E * (c + 1))
                    for t in range(TPC):
                        view = x_sb[:, TPC * c + t, :]
                        last = dve.tensor_tensor(view, psum[Y_BANKS[t]][:, 0:D], view, ALU.add)
                    last.then_inc(y_added, 1)

        @block.tensor
        def _(pe):
            def make(e):
                if places[e][1]:
                    pe.wait_ge(ring_read, places[e][1])
                return ring_bank(e)

            def make_side(e):
                i = side_at[e]
                if i >= ST_BANKS:
                    pe.wait_ge(side_read, i - ST_BANKS + 1)
                return side_bank(e)

            def contract(dst, lhs, rhs):
                for a in range(KD):
                    last = pe.matmul(dst, lhs(a), rhs(a), start=(a == 0), stop=(a == KD - 1))
                return last

            for e in plan:
                kind = e[0]
                if kind == "kq":
                    _, what, m, c = e
                    w = min(CH, KEYS - CH * c) if what == "k" else CH
                    if what == "k":
                        if c == 0:
                            pe.wait_ge(ld["wk"], 16)
                        pe.wait_ge(ld_ctx[c], 16)
                        wt, moving = wk_sb, ctx_sb[:, :, CH * c:CH * c + w]
                    else:
                        if c == 0:
                            pe.wait_ge(ld["wq"], 16)
                        pe.wait_ge(side_read, side_at[("xT0", c, 1)] + 1)
                        wt, moving = wq_sb, xn_t[:, c % 2, :, :]
                    bank = make(e)
                    contract(bank[:, 0:w], lambda a: wt[:, a, P * m:P * (m + 1)],
                             lambda a: moving[:, a, :]).then_inc(ring_full, 1)
                elif kind == "v":
                    t = e[1]
                    r = key_rows(t)
                    if t == 0:
                        pe.wait_ge(ld["wv"], 16)
                    bank = make_side(e)
                    contract(bank[0:r, 0:D], lambda a: ctx_sb[:, a, P * t:P * t + r],
                             lambda a: wv_sb[:, a, :]).then_inc(side_full, 1)
                elif kind in ("xT0", "xT1"):
                    _, c, half = e
                    first = kind == "xT0"
                    if first and c == 0:
                        pe.wait_ge(consts, 8)
                    pe.wait_ge(xn_ready, c + 1 if first else NC + c + 1)
                    bank = make_side(e) if first else make(e)
                    for t in range(2):
                        for a in range(KD):
                            last = pe.transpose(bank[:, P * (2 * t + a):P * (2 * t + a + 1)],
                                                xn_sb[:, 2 * half + t, P * a:P * (a + 1)], ident[:, :])
                    last.then_inc(side_full if first else ring_full, 1)
                elif kind == "gate":
                    _, c, half = e
                    if (c, half) == (0, 0):
                        pe.wait_ge(ld["wg"], 16)
                    bank = make(e)
                    for t in range(2):
                        tile = P * (2 * half + t)
                        last = contract(bank[:, D * t:D * (t + 1)], lambda a: xn_t[:, c % 2, a, tile:tile + P],
                                        lambda a: wg_sb[:, a, :])
                    last.then_inc(ring_full, 1)
                elif kind == "mx":
                    _, n, k = e
                    c, g = n // G, n % G
                    qt, h, k0, w, diagonal, _ = max_pieces(n)[k]
                    if k == 0:
                        if g == 0:
                            pe.wait_ge(q_landed[c], 16 * len(Q_PARTS))
                            pe.wait_ge(k_landed[c], 16 * len(K_PARTS))
                        if n == 0:
                            pe.wait_ge(bias_landed, 16)
                            pe.wait_ge(aug_q, 16)
                    bank = make(e)
                    d = P * (TPC * c + qt) - k0
                    for b0 in range(0, w, CH):
                        b1 = min(b0 + CH, w)
                        cut = diagonal and b0 <= d < b1
                        last = pe.matmul(bank[:, b0:b1], qaug[0:ROW_MAX, c % 2, 4 * g + h, P * qt:P * (qt + 1)],
                                         kaug[0:ROW_MAX, 4 * g + h, k0 + b0:k0 + b1], start=True, stop=not cut)
                        if cut:
                            last = pe.matmul(bank[:, d:b1], ident_b[:, :], tri_qk[:, 0:b1 - d], start=False, stop=True)
                    last.then_inc(ring_full, 1)
                elif kind == "mT":
                    n = e[1]
                    pe.wait_ge(nm_ready, n + 1)
                    bank = make(e)[0:8, 0:CH // 2].bitcast(BF16)
                    for t in range(TPC):
                        last = pe.transpose(bank[:, P * t:P * (t + 1)],
                                            nmax_b[:, n % 2, t, :, :].rearrange("p a h -> p (a h)"), ident_b[:, :])
                    last.then_inc(ring_full, 1)
                elif kind == "st":
                    _, u, n, j, h = e
                    c, g = n // G, n % G
                    i = st_at[(u, h)]
                    off = max(0, P * (j - TPC * c))
                    r = key_rows(j)
                    if j == 0 and h == 0:
                        pe.wait_ge(m_landed[n % 4], 32 * (n // 4 + 1))
                    if i == 0:
                        pe.wait_ge(side_read, len(side_at))
                    if i >= ST_BANKS:
                        pe.wait_ge(exp_done, i - ST_BANKS + 1)
                    bank = psum[i % ST_BANKS]
                    diagonal = j >= TPC * c
                    last = pe.matmul(bank[0:r, off:CH], kaug[0:ROWS, 4 * g + h, P * j:P * j + r],
                                     qaug[0:ROWS, c % 2, 4 * g + h, off:CH], start=True, stop=not diagonal)
                    if diagonal:
                        last = pe.matmul(bank[0:r, off:off + P], tri_qk[:, 0:r], ident_b[:, :], start=False, stop=True)
                    last.then_inc(st_full, 1)
                elif kind == "pv":
                    _, u, n, j = e
                    c, g = n // G, n % G
                    off = max(0, P * (j - TPC * c))
                    r = key_rows(j)
                    if j == 0 and n >= 1:
                        pe.wait_ge(o_copied, n)
                    pe.wait_ge(exp_done, st_at[(u, 3)] + 1)
                    for h in range(4):
                        col = (j * H + 4 * g + h) * VW
                        last = pe.matmul(psum[O_BANK][32 * h:32 * h + 32, off:CH], vaug[0:r, col:col + 32],
                                         probs[0:r, u % NSLOT, h, off:CH], start=(j == 0), stop=(j == key_tiles(c) - 1))
                    last.then_inc(pv_done, 1)
                elif kind == "oT":
                    n = e[1]
                    pe.wait_ge(o_copied, n + 1)
                    bank = make(e)
                    for t in range(TPC):
                        last = pe.transpose(bank[:, P * t:P * (t + 1)], o_sb[:, P * t:P * (t + 1)], ident[:, :])
                    last.then_inc(ring_full, 1)
                elif kind == "gT":
                    _, c, half = e
                    pe.wait_ge(gated, G * (c + 1))
                    bank = make(e)
                    for t in range(2):
                        for a in range(KD):
                            last = pe.transpose(bank[:, P * (2 * t + a):P * (2 * t + a + 1)],
                                                att_sb[:, 2 * half + t, P * a:P * (a + 1)], ident[:, :])
                    last.then_inc(ring_full, 1)
                elif kind == "wo":
                    _, c, half = e
                    if (c, half) == (0, 0):
                        pe.wait_ge(ld["wo"], 16)
                    pe.wait_ge(ring_read, ring_at[("gT", c, half)] + 1)
                    bank = make(e)
                    for t in range(2):
                        tile = P * (2 * half + t)
                        last = contract(bank[:, D * t:D * (t + 1)], lambda a: att_t[:, a, tile:tile + P],
                                        lambda a: wo_sb[:, a, :])
                    last.then_inc(ring_full, 1)
                elif kind == "logits":
                    c = e[1]
                    if c == 0:
                        pe.wait_ge(ld["gw"], 16)
                    pe.wait_ge(ring_read, ring_at[("xT1", c, 1)] + 1)
                    bank = make(e)
                    for t in range(TPC):
                        tile = P * t
                        last = contract(bank[:, E * t:E * (t + 1)], lambda a: gate_sb[:, c, CH * a + tile:CH * a + tile + P],
                                        lambda a: gw_sb[:, a, :])
                    last.then_inc(ring_full, 1)
                elif kind == "sT":
                    c = e[1]
                    pe.wait_ge(scale_ready, c + 1)
                    bank = make(e)
                    for t in range(TPC):
                        last = pe.transpose(bank[0:E, P * t:P * (t + 1)], scale_sb[:, t, :], ident[:, :])
                    last.then_inc(ring_full, 1)
                elif kind in ("a", "b"):
                    _, c, ex = e
                    if kind == "a":
                        if c == 0:
                            pe.wait_ge(w_lo_ready, ex + 1)
                        if ex == 0:
                            pe.wait_ge(x_lo_ready, c + 1)
                    part = 0 if kind == "a" else 1
                    bank = make(e)
                    for a in range(KD):
                        hi, lo = (w[:, ex, part, HID * a:HID * (a + 1)] for w in (w_hi, w_lo))
                        pe.matmul(bank[:, :], hi, x_hi[:, c % 2, a, :], start=(a == 0), stop=False)
                        pe.matmul(bank[:, :], hi, x_lo[c % 2][:, a, :], start=False, stop=False)
                        last = pe.matmul(bank[:, :], lo, x_hi[:, c % 2, a, :], start=False, stop=(a == KD - 1))
                    last.then_inc(ring_full, 1)
                elif kind == "y":
                    _, c, ex = e
                    i = c * E + ex
                    if i == 0:
                        pe.wait_ge(exp_done, len(st_at))
                        pe.wait_ge(o_copied, NC * G)
                    if ex == 0 and c:
                        pe.wait_ge(y_added, c)
                    pe.wait_ge(h_lo_ready, i + 1)
                    for t in range(TPC):
                        dst = psum[Y_BANKS[t]][:, 0:D]
                        hi, lo = (h[:, i % 2, P * t:P * (t + 1)] for h in (h_hi, h_lo))
                        pe.matmul(dst, hi, w_hi[:, ex, 2, :], start=(ex == 0), stop=False)
                        pe.matmul(dst, hi, w_lo[:, ex, 2, :], start=False, stop=False)
                        last = pe.matmul(dst, lo, w_hi[:, ex, 2, :], start=False, stop=(ex == E - 1))
                    last.then_inc(y_full, 1)


def kernel(x, ctx_1024, mask_BxS2_ik0, L0_xattn_Wq, L0_xattn_Wk, L0_xattn_Wv, L0_xattn_Wo, L0_xattn_Wg, L0_xattn_bg,
           L0_ffn_gate_w, L0_ffn_w1, L0_ffn_w2, L0_ffn_w3):
    import concourse.bacc as bacc
    from concourse.bass_utils import run_bass_kernel_spmd

    x, ctx_1024 = np.asarray(x), np.asarray(ctx_1024)
    arrays = {
        "x": x.reshape(TOK, D),
        "ctx_t": ctx_1024.reshape(KEYS, D).T,
        "mask": np.asarray(mask_BxS2_ik0).reshape(1, KEYS),
        "wq_t": np.asarray(L0_xattn_Wq).T,
        "wk_t": np.asarray(L0_xattn_Wk).T,
        "wv_t": np.asarray(L0_xattn_Wv).T,
        "wo_t": np.asarray(L0_xattn_Wo).T,
        "wg_t": np.asarray(L0_xattn_Wg).T,
        "bg": np.asarray(L0_xattn_bg),
        "gate_w": np.asarray(L0_ffn_gate_w),
        "w1": np.asarray(L0_ffn_w1),
        "w2": np.asarray(L0_ffn_w2),
        "w3": np.asarray(L0_ffn_w3),
    }
    arrays = {f"in_{k}": np.ascontiguousarray(a) for k, a in arrays.items()}
    nc = bacc.Bacc("TRN2", target_bir_lowering=False, num_devices=1)
    args = [nc.dram_tensor(k, a.shape, mybir.dt.from_np(a.dtype), kind="ExternalInput").ap() for k, a in arrays.items()]
    out = nc.dram_tensor("out", (TOK, D), F32, kind="ExternalOutput").ap()
    build(nc, *args, out)
    r = run_bass_kernel_spmd(nc, [arrays], core_ids=[0])
    return r.results[0]["out"].reshape(1, TOK, D)
```

```python
from contextlib import ExitStack

import numpy as np

import concourse.bass as bass
from concourse import mybir

F32 = mybir.dt.float32
BF16 = mybir.dt.bfloat16
F32R = mybir.dt.float32r
I32 = mybir.dt.int32
ALU = mybir.AluOpType
ACT = mybir.ActivationFunctionType
AX_X = mybir.AxisListType.X

P = 128
TOK, KEYS, D, H, DK = 2048, 1601, 256, 16, 16
E, HID = 8, 128
CH = 512
NC = TOK // CH
TPC = CH // P
NT = TOK // P
KT = (KEYS + P - 1) // P
KD = D // P
KP = 1602
G = H // 4
RING, RING0 = 4, 3
MAX_WIDTH = CH
ST_BANKS = 3
O_BANK = 7
NSLOT = 2
MASKED = -1.0e30
FLOOR = -1.0e20
TINY = 1.0e-30
EARLY_WS = 4
PACES = (1.13, 1.09, 1.05, 1.04)
MAX_MARGIN = 44
MAX_FOLD = 4
MAX_TURN = 16
LEAD = 35
AHEAD = (0, -30, -60, -30)
FIRST_STEPS = ["stat", "norm", "k0", "k1", "kload", "x0", "x1", "q0", "q1", "qload", "v04", "g0", "g1"]
NEXT_STEPS = ["stat", "k0", "k1", "kload", "norm", "v02", "x0", "x1", "q0", "q1", "qload", "v22", "g0", "g1", "sig"]
GT_AT, WO_AT, STAT_AT, NORM_AT, XT_AT, LOGITS_AT, REXP_AT, RANK_AT, ST_AT = 4, 4.75, 4.75, 8.25, 9.75, 10.75, 12.25, 13.25, 15.0
OT_AT = 0.75
XS_AT, WS_AT = 1, 4
GAP = 0.25
EPS = 1e-5
VW = DK + 1
Y_BANKS = (0, 1, 2, 7)
Q_PARTS = (0, 0, 0, 1, 1, 2)
K_PARTS = (0, 1, 2, 0, 1, 0)
ROW_MASK = len(Q_PARTS) * DK
ROW_MAX = ROW_MASK + 1
ROWS = ROW_MAX + 2


TWO_ONES = float(np.uint32(0x3F803F80).view(np.float32))


def key_tiles(c):
    return min(TPC * (c + 1), KT)


def key_rows(j):
    return min(P, KEYS - P * j)


def max_pieces(n):
    c, out = n // G, []
    for h in range(4):
        for qt in range(TPC):
            i = TPC * c + qt
            seen = min(P * (i + 1), KEYS)
            pieces = -(-seen // MAX_WIDTH)
            width = P * -(-(-(-seen // P)) // pieces)
            for slot in range(pieces):
                k0 = slot * width
                w = min(width, seen - k0)
                out.append((qt, h, k0, w, i < KT and k0 + w == seen, slot))
    return out


def max_schedule():
    tiles = [sum((CH - max(0, P * (j - TPC * (n // G)))) // P for j in range(key_tiles(n // G))) * 4 for n in range(NC * G)]
    starts = [sum(tiles[:n]) for n in range(NC * G)]
    events, end = [], float("inf")
    for n in reversed(range(NC * G)):
        end = min(end, starts[n] - MAX_MARGIN)
        pieces = max_pieces(n)
        total = sum(w / P for _, _, _, w, _, _ in pieces)
        pace = PACES[n // G]
        first = end - total / pace
        done = 0
        for k, (_, _, _, w, _, _) in enumerate(pieces):
            events.append((first + done / pace, n, 0, ("mx", n, k)))
            done += w / P
        events.append((end + MAX_FOLD, n, 1, ("mred", n)))
        events.append((end + MAX_TURN, n, 2, ("mT", n)))
        end = first
    events.sort()
    return [(at, e) for at, _, _, e in events]


def projections(c, order):
    steps = []
    for name in order:
        if name == "stat":
            steps.extend([("bn", 0, c), ("stat", 0, c)])
        elif name == "norm":
            steps.extend([("norm0", 0, c), ("norm", 0, c)])
        elif name in ("k0", "k1", "q0", "q1"):
            steps.append(("kq", name[0], int(name[1]), c))
        elif name in ("v04", "v02", "v22"):
            first = TPC * c + int(name[1])
            steps.extend([("v", t) for t in range(first, min(first + int(name[2]), KT))])
        elif name in ("x0", "x1"):
            steps.append(("xT0", c, int(name[1])))
        elif name in ("g0", "g1"):
            steps.append(("gate", c, int(name[1])))
        elif name == "qload":
            if c < 2:
                steps.append(("qload", c))
        elif name == "sig":
            steps.append(("sigmoid", c))
        else:
            steps.append(("kload", c))
    return steps


def untangle(plan):
    def norm_of(e):
        if e[0] in ("bn", "stat", "norm0", "norm"):
            return e[1:3]
        if e[0] in ("xT0", "gate", "sigmoid", "qload"):
            return (0, e[1])
        if e[0] == "kq" and e[1] == "q":
            return (0, e[3])
        if e[0] in ("xT1", "logits", "rexp", "rank0", "rank1", "rank", "sT"):
            return (1, e[1])
        return None

    out, waiting, now = [], [], None

    def put(e):
        nonlocal now
        which = norm_of(e)
        if which and ((e[0] == "bn" and now) or any(norm_of(w) == which for w in waiting)):
            waiting.append(e)
            return
        out.append(e)
        if e[0] == "bn":
            now = which
        elif e[0] in ("xT0", "xT1") and e[2] == 1:
            now = None
            again = waiting[:]
            waiting.clear()
            for w in again:
                put(w)

    for e in plan:
        put(e)
    for c in range(2, NC):
        at, made = out.index(("qload", c)), out.index(("kq", "q", 1, c))
        if at < made:
            out.insert(made + 1, out[at])
            del out[at]
    return out


def make_plan():
    plan, due = [], []

    def later(unit, *events):
        due.extend((unit, e) for e in events)

    def emit_due(unit):
        now = [e for u, e in due if u <= unit]
        due[:] = [(u, e) for u, e in due if u > unit]
        plan.extend(now)

    schedule = max_schedule()
    plan.extend(projections(0, FIRST_STEPS))
    start = schedule[0][0]
    for c in range(1, NC):
        end = min(at for at, e in schedule if e[0] == "mx" and e[1] == G * c) - LEAD
        steps = projections(c, NEXT_STEPS)
        start += AHEAD[c]
        schedule.extend((start + (end - start) * i / len(steps), e) for i, e in enumerate(steps))
        start = end
    schedule.append((start, ("prologue_end",)))
    schedule.sort(key=lambda s: s[0])
    while schedule[0][0] < 0:
        plan.append(schedule.pop(0)[1])

    units = [(n, j) for n in range(NC * G) for j in range(key_tiles(n // G))]
    position = 0

    def after_chunk(c, u):
        later(u + GT_AT, ("gT", c, 0), ("gT", c, 1))
        later(u + WO_AT, ("wo", c, 0), ("wo", c, 1))
        later(u + STAT_AT, ("bn", 1, c))
        later(u + STAT_AT + GAP, ("stat", 1, c))
        later(u + NORM_AT, ("norm0", 1, c))
        later(u + NORM_AT + GAP, ("norm", 1, c))
        later(u + XT_AT, ("xT1", c, 0), ("xT1", c, 1))
        later(u + LOGITS_AT, ("logits", c))
        later(u + REXP_AT, ("rexp", c))
        later(u + RANK_AT, ("rank0", c))
        later(u + RANK_AT + GAP, ("rank1", c))
        later(u + RANK_AT + 2 * GAP, ("rank", c))
        later(u + ST_AT, ("sT", c))

    for u, (n, j) in enumerate(units):
        for h in range(4):
            emit_due(u - 1 + h / 4)
            while schedule and schedule[0][0] <= position:
                plan.append(schedule.pop(0)[1])
            plan.append(("st", u, n, j, h))
            position += (CH - max(0, P * (j - TPC * (n // G)))) // P
            if u > 0 and h == 3:
                plan.append(("pv", u - 1, *units[u - 1]))
        emit_due(u)
        if u > 0 and units[u - 1][0] != n:
            m = n - 1
            plan.append(("ocopy", m))
            later(u + OT_AT, ("oT", m))
            if m % G == G - 1:
                after_chunk(m // G, u)
                if m // G + 2 < NC:
                    plan.append(("qload", m // G + 2))
                if m // G == 2:
                    later(u + 1, ("sload", 0))
            if n == NC * G - 1:
                later(u + XS_AT, ("xs", 0))
                for ex in range(EARLY_WS):
                    later(u + WS_AT + ex, ("ws", ex))
    u = len(units)
    plan.append(("pv", u - 1, *units[u - 1]))
    later(u, ("ocopy", NC * G - 1), ("oT", NC * G - 1))
    after_chunk(NC - 1, u - 3)
    todo = [(c, e) for c in range(NC) for e in range(E)]
    for i, (c, e) in enumerate(todo):
        if i == 1:
            later(u, ("sload", 1))
        if c == 0 and EARLY_WS <= e + 3 < E:
            plan.append(("ws", e + 3))
        if i:
            plan.append(("hl", *todo[i - 1]))
        plan.append(("a", c, e))
        plan.extend([("b", c, e), ("h", c, e)])
        if e == 5 and c + 1 < NC:
            plan.append(("xs", c + 1))
        emit_due(u)
        u += 1
        if i:
            plan.append(("y", *todo[i - 1]))
            if e == 0:
                plan.append(("out", c - 1))
                if c + 1 < NC:
                    plan.append(("sload", c + 1))
    plan.extend([("hl", *todo[-1]), ("y", *todo[-1]), ("out", NC - 1)])
    return untangle(plan), units


RING_KINDS = ("gate", "mx", "mT", "oT", "wo", "logits", "sT", "a", "b")


def ring_places(items):
    places, owner, at = {}, [0] * RING, 0
    for i, e in enumerate(items):
        banks = 2 if e[0] == "mx" and max_pieces(e[1])[e[2]][3] > CH else 1
        if banks == 2:
            at += at % 2
        mine = [(at + k) % RING for k in range(banks)]
        places[e] = (mine[0], max(owner[k] for k in mine))
        for k in mine:
            owner[k] = i + 1
        at += banks
    return places


SIDE_KINDS = ("kq", "v", "xT0", "st")


def by_side(e):
    return e[0] in SIDE_KINDS or e[0] in ("gT", "xT1") and e[1] < NC - 1


def by_ring(e):
    return e[0] in RING_KINDS or e[0] in ("gT", "xT1") and e[1] == NC - 1



def build(nc, x, ctx_t, mask, wq_t, wk_t, wv_t, wo_t, wg_t, bg, gate_w, w1, w2, w3, out):
    plan, units = make_plan()
    ring_at = {e: i for i, e in enumerate([e for e in plan if by_ring(e)])}
    places = ring_places(list(ring_at))
    side_at = {e: i for i, e in enumerate([e for e in plan if by_side(e)])}
    kq_at = {e: i for i, e in enumerate([e for e in plan if e[0] == "kq"])}
    st_at = {(e[1], e[4]): i for e, i in side_at.items() if e[0] == "st"}
    norm_at = {e[1:]: i for i, e in enumerate([e for e in plan if e[0] == "norm"])}
    early_side = max(i for e, i in side_at.items() if e[0] in ("kq", "v", "xT0")) + 1
    last_unit = {n: u for u, (n, _) in enumerate(units)}
    last_st = {}
    for u, (n, _) in enumerate(units):
        last_st[n // G] = st_at[(u, 3)]
    prologue_items = max(i for e, i in ring_at.items() if e[0] == "gate") + 1

    with ExitStack() as ctx:
        def sb(name, shape, dt, stack=ctx):
            return stack.enter_context(nc.sbuf_tensor(name, shape, dt))

        def sem(name):
            return ctx.enter_context(nc.semaphore(name))

        def scratch(name, shape, dt):
            return nc.dram_tensor(name, shape, dt, kind="Internal").ap()

        k_parts = scratch("k_parts", (3, D, KEYS), BF16)
        q_parts = scratch("q_parts", (3, D, TOK), BF16)
        s_dram = scratch("s_dram", (E, TOK), F32)

        x_sb = sb("x_sb", [P, NT, D], F32)
        gate_sb = sb("gate_sb", [P, NC, TPC * D], F32)
        qaug = sb("qaug", [P, 2, H, CH], BF16)
        vaug = sb("vaug", [P, KT * H * VW + 16], F32)
        with ExitStack() as attention:
            kaug = sb("kaug", [P, H, KP], BF16, attention)
            probs = sb("probs", [P, NSLOT, 4, CH], F32, attention)
        w_hi = sb("w_hi", [P, E, 3, D], F32R)
        w_lo = sb("w_lo", [P, E, 3, D], F32R)
        h_hi = sb("h_hi", [P, 2, CH], F32R)
        h_lo = sb("h_lo", [P, 2, CH], F32R)
        u_sb = sb("u_sb", [P, 2, CH], F32)
        v_sb = sb("v_sb", [P, 2, CH], F32)
        x_lo1 = sb("x_lo1", [P, KD, CH], F32R)
        o_sb = sb("o_sb", [P, CH], F32)
        att_sb = sb("att_sb", [P, TPC, D], F32)
        att_t = sb("att_t", [P, KD, CH], F32)
        xn_sb = sb("xn_sb", [P, TPC, D], F32)
        wo_sb = sb("wo_sb", [P, KD, D], F32)
        gw_sb = sb("gw_sb", [P, KD, E], F32)
        ident = sb("ident", [P, P], F32)
        ident_b = sb("ident_b", [P, P], BF16)
        zero_b = sb("zero_b", [P, P], BF16)
        tri_qk = sb("tri_qk", [P, P], BF16)
        lower = sb("lower", [P, E, E], F32)
        ones_f = sb("ones_f", [P, E, E], F32)
        pmax = sb("pmax", [P, 2, TPC, 4, 4], F32)
        rmax = sb("rmax", [P, 2, TPC * 4], F32)
        nmax = sb("nmax", [P, 2, TPC * 4], F32)
        nmax_b = sb("nmax_b", [P, 2, TPC, 2, 4], BF16)
        m_row = sb("m_row", [8, 2, CH], BF16)
        stat6 = sb("stat6", [P, TPC, 6], F32)
        stat2 = sb("stat2", [P, TPC, 2], F32)
        var_e = sb("var_e", [P, TPC], F32)
        rstd = sb("rstd", [P, TPC], F32)
        minus_half = sb("minus_half", [P, TPC], F32)
        rsum = sb("rsum", [P, TPC, 4], F32)
        rinv = sb("rinv", [P, TPC, 4], F32)
        r_max = sb("r_max", [P, TPC], F32)
        r_log = sb("r_log", [P, TPC, E], F32)
        r_exp = sb("r_exp", [P, TPC, E], F32)
        r_sum = sb("r_sum", [P, TPC], F32)
        r_inv = sb("r_inv", [P, TPC], F32)
        r_prob = sb("r_prob", [P, TPC, E], F32)
        r_gt, r_eq = (att_t[:, a, 0:TPC * E * E].rearrange("p (t i j) -> p t i j", t=TPC, i=E) for a in (0, 1))
        r_rank = sb("r_rank", [P, TPC, E], F32)
        scale_sb = sb("scale_sb", [P, TPC, E], F32)
        sT_sb = sb("sT_sb", [E, CH], F32)
        with ExitStack() as early:
            ctx_sb = sb("ctx_sb", [P, KD, KEYS], F32, early)
            wq_sb = sb("wq_sb", [P, KD, D], F32, early)
            wk_sb = sb("wk_sb", [P, KD, D], F32, early)
            wv_sb = sb("wv_sb", [P, KD, D], F32, early)
            wg_sb = sb("wg_sb", [P, KD, D], F32, early)
            xn_t = sb("xn_t", [P, KD, CH], F32, early)
            bg_sb = sb("bg_sb", [P, D], F32, early)
            stage = [sb(f"stage{s}", [P, 3, CH], BF16, early) for s in range(2)]
            rest = [sb(f"rest{s}", [P, CH], F32, early) for s in range(2)]
        w_sb = sb("w_sb", [P, E, 3, D], F32)
        x_hi = sb("x_hi", [P, 2, KD, CH], F32R)
        x_lo0 = sb("x_lo0", [P, KD, CH], F32R)
        x_lo = (x_lo0, x_lo1)
        words = probs[:, :, :, :].rearrange("p s h q -> p (s h q)")
        mask_i = words[0:1, 2 * CH * 2:2 * CH * 2 + KEYS].bitcast(I32)
        scale_bc = [qaug[:, s, :, :].rearrange("p h q -> p (h q)").bitcast(F32).rearrange("p (e q) -> p e q", e=E)
                    for s in range(2)]
        vflat = vaug[:, 0:KT * H * VW].rearrange("p (t h w) -> p t h w", t=KT, h=H)
        ones_row = words[0:ROWS - ROW_MASK, 0:KP // 2].bitcast(BF16)
        bias_row = words[0:1, 2 * CH:2 * CH + KP // 2].bitcast(BF16)[:, 0:KEYS]

        psum = {i: ctx.enter_context(nc.psum_tensor(f"bank{i}", [P, CH], F32)) for i in range(RING0)}
        ring = ctx.enter_context(nc.psum_tensor("ring", [P, RING * CH], F32))
        psum[O_BANK] = ctx.enter_context(nc.psum_tensor(f"bank{O_BANK}", [P, CH], F32))

        def side_bank(e):
            return psum[side_at[e] % ST_BANKS]

        def ring_bank(e):
            first = places[e][0]
            return ring[:, CH * first:CH * (first + (2 if e[0] == "mx" and first % 2 == 0 else 1))]

        def taken(e):
            return (side_read, side_at[e] + 1) if by_side(e) else (ring_read, ring_at[e] + 1)

        def made(e):
            return (side_full, side_at[e] + 1) if by_side(e) else (ring_full, ring_at[e] + 1)

        ld = {k: sem(f"ld_{k}") for k in ("wk", "wq", "wv", "wg", "bg", "wo", "gw", "mask", "w1", "w3", "w2")}
        ld_ctx = [sem(f"ld_ctx{i}") for i in range(NC)]
        ld_x = [sem(f"ld_x{i}") for i in range(NC)]
        consts = sem("consts")
        aug_src = sem("aug_src")
        aug_k = sem("aug_k")
        aug_q = sem("aug_q")
        v_ones = sem("v_ones")
        pmax_set = sem("pmax_set")
        bias_ready = sem("bias_ready")
        bias_landed = sem("bias_landed")
        ring_full = sem("ring_full")
        ring_read = sem("ring_read")
        hi_ready = sem("hi_ready")
        rest_ready = sem("rest_ready")
        mid_ready = sem("mid_ready")
        lo_ready = sem("lo_ready")
        parts_out = [sem(f"parts_out{i}") for i in range(2)]
        k_landed = [sem(f"k_landed{i}") for i in range(NC)]
        q_landed = [sem(f"q_landed{i}") for i in range(NC)]
        var_ready = sem("var_ready")
        rstd_ready = sem("rstd_ready")
        side_full = sem("side_full")
        side_read = sem("side_read")
        xn_ready = sem("xn_ready")
        gate_ready = sem("gate_ready")
        pv_done = sem("pv_done")
        mx_reduced = sem("mx_reduced")
        nm_ready = sem("nm_ready")
        nm_step = sem("nm_step")
        m_landed = [sem(f"m_landed{i}") for i in range(4)]
        o_copied = sem("o_copied")
        gated = sem("gated")
        r_log_ready = sem("r_log_ready")
        r_exp_ready = sem("r_exp_ready")
        scale_ready = sem("scale_ready")
        s_stored = [sem(f"s_stored{i}") for i in range(NC)]
        s_landed = [sem(f"s_landed{i}") for i in range(NC)]
        w_hi_ready = sem("w_hi_ready")
        w_lo_ready = sem("w_lo_ready")
        x_hi_ready = sem("x_hi_ready")
        x_lo_ready = sem("x_lo_ready")
        silu_done = sem("silu_done")
        h_ready = sem("h_ready")
        h_hi_ready = sem("h_hi_ready")
        h_lo_ready = sem("h_lo_ready")
        y_full = sem("y_full")
        y_added = sem("y_added")
        out_done = sem("out_done")
        dve_step = sem("dve_step")
        block = ctx.enter_context(nc.Block())

        def lower_parts(engine, e):
            i, (_, what, m, c) = kq_at[e], e
            w = min(CH, KEYS - CH * c) if what == "k" else CH
            parts, left = stage[i % 2], rest[i % 2][:, 0:w]
            engine.wait_ge(hi_ready, i + 1)
            engine.wait_ge(side_read, side_at[e] + 1)
            engine.tensor_tensor(left, left, parts[:, 0, 0:w], ALU.subtract).then_inc(rest_ready, 1)
            engine.wait_ge(rest_ready, i + 1)
            engine.tensor_copy(parts[:, 1, 0:w], left).then_inc(mid_ready, 1)
            engine.wait_ge(mid_ready, i + 1)
            engine.tensor_tensor(parts[:, 2, 0:w], left, parts[:, 1, 0:w], ALU.subtract).then_inc(lo_ready, 1)

        @block.sync
        def _(sp):
            def tiles(w):
                return w.rearrange("(a p) n -> p a n", p=P)

            sp.dma_start(wk_sb[:, :, :], tiles(wk_t)).then_inc(ld["wk"], 16)
            last_rows = ROWS - ROW_MASK
            for c in range(NC):
                k0, k1 = CH * c, min(CH * (c + 1), KEYS)
                sp.dma_start(ctx_sb[:, :, k0:k1], tiles(ctx_t)[:, :, k0:k1]).then_inc(ld_ctx[c], 16)
                if c == 0:
                    sp.dma_start(wq_sb[:, :, :], tiles(wq_t)).then_inc(ld["wq"], 16)
            for name, dst, src in (("wg", wg_sb, wg_t), ("wo", wo_sb, wo_t), ("gw", gw_sb, gate_w)):
                sp.dma_start(dst[:, :, :], tiles(src)).then_inc(ld[name], 16)
            sp.wait_ge(aug_src, 1)
            sp.dma_start(kaug[ROW_MASK:ROWS, :, :], ones_row.unsqueeze(1).to_broadcast([last_rows, H, KP])).then_inc(aug_k, 16)
            sp.dma_start(qaug[ROW_MASK:ROWS, :, :, :].rearrange("p s h q -> p (s h) q"),
                         ones_row[:, 0:CH].unsqueeze(1).to_broadcast([last_rows, 2 * H, CH])).then_inc(aug_q, 16)
            for e in plan:
                kind = e[0]
                if kind == "kq":
                    i, (_, what, m, c) = kq_at[e], e
                    w = min(CH, KEYS - CH * c) if what == "k" else CH
                    parts = k_parts if what == "k" else q_parts
                    sp.wait_ge(hi_ready, i + 1)
                    sp.wait_ge(mid_ready, i + 1)
                    sp.wait_ge(lo_ready, i + 1)
                    sp.dma_start(parts[:, P * m:P * (m + 1), CH * c:CH * c + w].rearrange("a p q -> p a q"),
                                 stage[i % 2][:, :, 0:w]).then_inc(parts_out[i % 2], 16)
                elif kind in ("kload", "qload"):
                    c, what = e[1], kind[0]
                    i = kq_at[("kq", what, 1, c)]
                    sp.wait_ge(parts_out[i % 2], 16 * (i // 2 + 1))
                    sp.wait_ge(parts_out[(i - 1) % 2], 16 * ((i - 1) // 2 + 1))
                    if what == "q" and c >= 2:
                        sp.wait_ge(side_full, last_st[c - 2] + 1)
                    w = min(CH, KEYS - CH * c) if what == "k" else CH
                    for r in range(len(Q_PARTS)):
                        if what == "k":
                            dst = kaug[DK * r:DK * (r + 1), :, CH * c:CH * c + w]
                            src = k_parts[K_PARTS[r], :, CH * c:CH * c + w]
                        else:
                            dst = qaug[DK * r:DK * (r + 1), c % 2, :, :]
                            src = q_parts[Q_PARTS[r], :, CH * c:CH * c + w]
                        sp.dma_start(dst, src.rearrange("(h d) q -> d h q", d=DK)
                                     ).then_inc((k_landed if what == "k" else q_landed)[c], 16)
                    if what == "k" and c == 0:
                        sp.wait_ge(aug_k, 16)
                        sp.wait_ge(bias_ready, 1)
                        sp.dma_start(kaug[ROW_MASK:ROW_MASK + 1, :, 0:KEYS],
                                     bias_row.unsqueeze(1).to_broadcast([1, H, KEYS])).then_inc(bias_landed, 16)
                elif kind == "mT":
                    n = e[1]
                    c, g = n // G, n % G
                    sp.wait_ge(ring_read, ring_at[e] + 1)
                    sp.wait_ge(aug_q, 16)
                    for part in range(2):
                        sp.dma_start(qaug[ROW_MAX + part:ROW_MAX + part + 1, c % 2, 4 * g:4 * g + 4, :],
                                     m_row[4 * part:4 * part + 4, n % 2, :]).then_inc(m_landed[n % 4], 16)
                elif kind == "prologue_end":
                    sp.wait_ge(ring_full, prologue_items)
                    sp.wait_ge(ring_read, prologue_items)
                    sp.wait_ge(side_read, early_side)
                    for s in range(2):
                        sp.wait_ge(parts_out[s], 16 * (len(kq_at) // 2))
                    for part, name, src in ((0, "w1", w1), (1, "w3", w3)):
                        dst = w_sb[:, :, part, :].rearrange("p e (a h) -> p e a h", a=KD)
                        for a in range(KD):
                            sp.dma_start(dst[:, :, a, :], src[:, P * a:P * (a + 1), :].rearrange("e p h -> p e h")
                                         ).then_inc(ld[name], 16)
                    sp.dma_start(w_sb[:, :, 2, :], w2.rearrange("e h d -> h e d")).then_inc(ld["w2"], 16)
                elif kind == "sT":
                    c = e[1]
                    sp.wait_ge(ring_read, ring_at[e] + 1)
                    sp.dma_start(s_dram[:, CH * c:CH * (c + 1)], sT_sb[:, :]).then_inc(s_stored[c], 16)
                elif kind == "sload":
                    c = e[1]
                    sp.wait_ge(s_stored[c], 16)
                    if c == 0:
                        sp.wait_ge(side_full, last_st[2] + 1)
                    elif c == 1:
                        sp.wait_ge(side_full, last_st[3] + 1)
                    else:
                        sp.wait_ge(ring_read, ring_at[("b", c - 2, E - 1)] + 1)
                    sp.dma_start(scale_bc[c % 2], s_dram[:, CH * c:CH * (c + 1)].partition_broadcast(P)
                                 ).then_inc(s_landed[c], 16)
                elif kind == "out":
                    c = e[1]
                    sp.wait_ge(y_added, c + 1)
                    sp.dma_start(out.rearrange("(t p) d -> p t d", p=P)[:, TPC * c:TPC * (c + 1), :],
                                 x_sb[:, TPC * c:TPC * (c + 1), :]).then_inc(out_done, 16)
            sp.wait_ge(out_done, 16 * NC)

        @block.gpsimd
        def _(pool):
            def select(dst, src, pattern, base, mult, op, fill):
                return pool.affine_select(out=dst, in_=src, compare_op=op, fill=fill, base=base,
                                          pattern=pattern, channel_multiplier=mult)

            pool.memset(ones_row.bitcast(F32), TWO_ONES).then_inc(aug_src, 1)
            pool.memset(zero_b[:, :], 0.0).then_inc(consts, 1)
            pool.memset(ident[:, :], 0.0).then_inc(consts, 1)
            pool.memset(ones_f[:, :, :], 1.0).then_inc(consts, 1)
            pool.memset(minus_half[:, :], -0.5).then_inc(consts, 1)
            pool.wait_ge(consts, 4)
            select(ident[:, :], ident[:, :], [[-1, P]], 0, 1, ALU.not_equal, 1.0).then_inc(consts, 1)
            select(ident_b[:, :], zero_b[:, :], [[-1, P]], 0, 1, ALU.not_equal, 1.0).then_inc(consts, 1)
            select(tri_qk[:, :], zero_b[:, :], [[-1, P]], 0, 1, ALU.is_ge, MASKED).then_inc(consts, 1)
            select(lower[:, :, :], ones_f[:, :, :], [[1, E], [-1, E]], 0, 0, ALU.is_gt, 0.0).then_inc(consts, 1)
            pool.memset(vaug[:, :], 1.0).then_inc(v_ones, 1)
            norms = 0
            for e in plan:
                kind = e[0]
                if kind == "stat":
                    norms += 1
                    pool.wait_ge(var_ready, norms)
                    if norms > 1:
                        pool.wait_ge(xn_ready, norms - 1)
                    pool.tensor_tensor(rstd[:, :], var_e[:, :], minus_half[:, :], ALU.pow).then_inc(rstd_ready, 1)
                elif kind == "kq":
                    if e[3]:
                        lower_parts(pool, e)
                elif kind == "mred":
                    n = e[1]
                    s = n % 2
                    view = nmax[:, s, :].rearrange("p (t h) -> p t h", t=TPC)
                    pool.wait_ge(mx_reduced, n + 1)
                    if n >= 2:
                        pool.wait_ge(ring_read, ring_at[("mT", n - 2)] + 1)
                    pool.tensor_scalar(nmax[:, s, :], rmax[:, s, :], FLOOR, -1.0, ALU.max, ALU.mult).then_inc(nm_step, 1)
                    pool.wait_ge(nm_step, 2 * n + 1)
                    pool.tensor_copy(nmax_b[:, s, :, 0, :], view).then_inc(nm_step, 1)
                    pool.wait_ge(nm_step, 2 * n + 2)
                    pool.tensor_tensor(nmax_b[:, s, :, 1, :], view, nmax_b[:, s, :, 0, :], ALU.subtract).then_inc(nm_ready, 1)
                elif kind == "oT":
                    n = e[1]
                    c, g = n // G, n % G
                    view = att_sb[:, :, 64 * g:64 * (g + 1)]
                    pool.wait_ge(ring_read, ring_at[e] + 1)
                    pool.wait_ge(gate_ready, c + 1)
                    pool.tensor_tensor(view, view,
                                       gate_sb[:, c, :].rearrange("p (t d) -> p t d", t=TPC)[:, :, 64 * g:64 * (g + 1)],
                                       ALU.mult).then_inc(gated, 1)

        @block.scalar
        def _(act):
            xv = x.rearrange("(t p) d -> p t d", p=P)
            act.dma_start(x_sb[:, 0:TPC, :], xv[:, 0:TPC, :]).then_inc(ld_x[0], 16)
            act.dma_start(mask_i[:, :], mask).then_inc(ld["mask"], 16)
            act.dma_start(wv_sb[:, :, :], wv_t.rearrange("(a p) n -> p a n", p=P)).then_inc(ld["wv"], 16)
            act.dma_start(bg_sb[:, :], bg.partition_broadcast(P)).then_inc(ld["bg"], 16)
            for c in range(1, NC):
                act.dma_start(x_sb[:, TPC * c:TPC * (c + 1), :], xv[:, TPC * c:TPC * (c + 1), :]).then_inc(ld_x[c], 16)
            for e in plan:
                kind = e[0]
                if kind == "kq":
                    i, (_, what, m, c) = kq_at[e], e
                    w = min(CH, KEYS - CH * c) if what == "k" else CH
                    act.wait_ge(side_full, side_at[e] + 1)
                    if i >= 2:
                        act.wait_ge(parts_out[i % 2], 16 * (i // 2))
                    act.activation(stage[i % 2][:, 0, 0:w], side_bank(e)[:, 0:w], ACT.Copy).then_inc(hi_ready, 1)
                    act.activation(rest[i % 2][:, 0:w], side_bank(e)[:, 0:w], ACT.Copy).then_inc(side_read, 1)
                elif kind == "v":
                    t = e[1]
                    r = key_rows(t)
                    if t == 0:
                        act.wait_ge(v_ones, 1)
                    act.wait_ge(side_full, side_at[e] + 1)
                    act.activation(vflat[0:r, t, :, 0:DK], side_bank(e)[0:r, 0:D].rearrange("p (h d) -> p h d", h=H),
                                   ACT.Copy).then_inc(side_read, 1)
                elif kind == "xT0":
                    _, c, half = e
                    if c:
                        act.wait_ge(ring_full, ring_at[("gate", c - 1, 1)] + 1)
                    act.wait_ge(side_full, side_at[e] + 1)
                    dst = xn_t[:, :, :].rearrange("p a (t q) -> p t a q", q=P)[:, 2 * half:2 * half + 2, :, :]
                    act.activation(dst, side_bank(e)[:, :].rearrange("p (t a q) -> p t a q", t=2, a=KD),
                                   ACT.Copy).then_inc(side_read, 1)
                elif kind == "xT1" and by_side(e):
                    _, c, half = e
                    act.wait_ge(gated, G * (c + 1))
                    act.wait_ge(side_full, side_at[e] + 1)
                    dst = gate_sb[:, c, :].rearrange("p (a t q) -> p t a q", a=KD, q=P)[:, 2 * half:2 * half + 2, :, :]
                    act.activation(dst, side_bank(e)[:, :].rearrange("p (t a q) -> p t a q", t=2, a=KD),
                                   ACT.Copy).then_inc(side_read, 1)
                elif kind == "gT" and by_side(e):
                    _, c, half = e
                    if c:
                        act.wait_ge(ring_full, ring_at[("wo", c - 1, 1)] + 1)
                        act.wait_ge(scale_ready, c)
                    act.wait_ge(side_full, side_at[e] + 1)
                    dst = att_t[:, :, :].rearrange("p a (t q) -> p t a q", q=P)[:, 2 * half:2 * half + 2, :, :]
                    act.activation(dst, side_bank(e)[:, :].rearrange("p (t a q) -> p t a q", t=2, a=KD),
                                   ACT.Copy).then_inc(side_read, 1)
                elif kind == "sigmoid":
                    for c in (0, 1) if e[1] == 1 else (e[1],):
                        act.wait_ge(ring_read, ring_at[("gate", c, 1)] + 1)
                        act.activation(gate_sb[:, c, :], gate_sb[:, c, :], ACT.Sigmoid).then_inc(gate_ready, 1)
                elif kind == "ocopy":
                    n = e[1]
                    act.wait_ge(pv_done, last_unit[n] + 1)
                    if n >= 1:
                        act.wait_ge(ring_full, ring_at[("oT", n - 1)] + 1)
                    act.activation(o_sb[:, :], psum[O_BANK][:, :], ACT.Copy).then_inc(o_copied, 1)
                elif kind == "st":
                    _, u, n, j, h = e
                    i = st_at[(u, h)]
                    off = max(0, P * (j - TPC * (n // G)))
                    rows = key_rows(j)
                    if u == 0 and h == 0:
                        act.wait_ge(aug_k, 16)
                        act.wait_ge(aug_q, 16)
                        act.wait_ge(bias_landed, 16)
                    act.wait_ge(side_full, i + 1)
                    if u >= NSLOT:
                        act.wait_ge(pv_done, u - NSLOT + 1)
                    act.activation(probs[0:rows, u % NSLOT, h, off:CH], side_bank(e)[0:rows, off:CH], ACT.Exp,
                                   scale=DK ** -0.5).then_inc(side_read, 1)
                elif kind == "rexp":
                    c = e[1]
                    act.wait_ge(r_log_ready, c + 1)
                    act.activation(r_exp[:, :, :], r_log[:, :, :], ACT.Exp).then_inc(r_exp_ready, 1)
                elif kind == "ws" and e[1] >= EARLY_WS:
                    ex = e[1]
                    if ex == EARLY_WS:
                        for name, times in (("w1", KD), ("w3", KD), ("w2", 1)):
                            act.wait_ge(ld[name], 16 * times)
                        act.wait_ge(pv_done, len(units))
                    act.activation(w_hi[:, ex, :, :], w_sb[:, ex, :, :], ACT.Copy).then_inc(w_hi_ready, 1)
                elif kind == "xs" and e[1]:
                    c = e[1]
                    act.wait_ge(*taken(("xT1", c, 1)))
                    if c >= 2:
                        act.wait_ge(ring_full, ring_at[("b", c - 2, E - 1)] + 1)
                    act.activation(x_hi[:, c % 2, :, :], gate_sb[:, c, :].rearrange("p (a q) -> p a q", a=KD),
                                   ACT.Copy).then_inc(x_hi_ready, 1)
                elif kind == "h":
                    _, c, ex = e
                    i = c * E + ex
                    act.wait_ge(ring_read, ring_at[("a", c, ex)] + 1)
                    act.activation(u_sb[:, i % 2, :], u_sb[:, i % 2, :], ACT.Silu).then_inc(silu_done, 1)
                elif kind == "hl":
                    _, c, ex = e
                    i = c * E + ex
                    act.wait_ge(h_ready, i + 1)
                    if i >= 2:
                        act.wait_ge(y_full, i - 1)
                    act.activation(h_hi[:, i % 2, :], v_sb[:, i % 2, :], ACT.Copy).then_inc(h_hi_ready, 1)

        @block.vector
        def _(dve):
            steps = [0]

            def step(ins):
                ins.then_inc(dve_step, 1)
                steps[0] += 1
                dve.wait_ge(dve_step, steps[0])

            dve.memset(pmax[:, :, :, :, :], MASKED).then_inc(pmax_set, 1)
            dve.wait_ge(pmax_set, 1)
            norms = 0
            for e in plan:
                kind = e[0]
                if by_ring(e):
                    dve.wait_ge(ring_full, ring_at[e] + 1)
                    bank = ring_bank(e)
                if kind == "kq" and e[3] == 0:
                    lower_parts(dve, e)
                elif kind == "bn":
                    _, second, c = e
                    if not second:
                        dve.wait_ge(ld_x[c], 16)
                    else:
                        dve.wait_ge(ring_read, ring_at[("wo", c, 1)] + 1)
                    for t in (0, 1):
                        last = dve.bn_stats(stat6[:, t, :], x_sb[:, TPC * c + t, :])
                    step(last)
                elif kind == "stat":
                    _, second, c = e
                    for t in (2, 3):
                        last = dve.bn_stats(stat6[:, t, :], x_sb[:, TPC * c + t, :])
                    step(last)
                    for t in range(TPC):
                        last = dve.bn_aggr(stat2[:, t, :], stat6[:, t, :])
                    step(last)
                    dve.tensor_scalar(var_e[:, :], stat2[:, :, 1], EPS, None, ALU.add).then_inc(var_ready, 1)
                elif kind == "norm0":
                    _, second, c = e
                    norms += 1
                    dve.wait_ge(rstd_ready, norms)
                    if norms > 1:
                        was_second, was = next(k for k, i in norm_at.items() if i == norms - 2)
                        if was_second:
                            dve.wait_ge(*made(("xT1", was, 1)))
                        else:
                            dve.wait_ge(side_full, side_at[("xT0", was, 1)] + 1)
                    for t in (0, 1):
                        dve.tensor_scalar(xn_sb[:, t, :], x_sb[:, TPC * c + t, :], stat2[:, t, 0:1],
                                          rstd[:, t:t + 1], ALU.subtract, ALU.mult)
                elif kind == "norm":
                    _, second, c = e
                    for t in (2, 3):
                        last = dve.tensor_scalar(xn_sb[:, t, :], x_sb[:, TPC * c + t, :], stat2[:, t, 0:1],
                                                 rstd[:, t:t + 1], ALU.subtract, ALU.mult)
                    last.then_inc(xn_ready, 1)
                    if (second, c) == (0, 0):
                        dve.wait_ge(ld["mask"], 16)
                        dve.tensor_scalar(bias_row, mask_i[:, :], 0, MASKED, ALU.is_equal, ALU.mult).then_inc(bias_ready, 1)
                elif kind == "xT1" and by_ring(e):
                    _, c, half = e
                    dve.wait_ge(gated, G * (c + 1))
                    dst = gate_sb[:, c, :].rearrange("p (a t q) -> p t a q", a=KD, q=P)[:, 2 * half:2 * half + 2, :, :]
                    dve.tensor_copy(dst, bank[:, :].rearrange("p (t a q) -> p t a q", t=2, a=KD)).then_inc(ring_read, 1)
                elif kind == "gT" and by_ring(e):
                    _, c, half = e
                    dve.wait_ge(ring_full, ring_at[("wo", c - 1, 1)] + 1)
                    dst = att_t[:, :, :].rearrange("p a (t q) -> p t a q", q=P)[:, 2 * half:2 * half + 2, :, :]
                    dve.tensor_copy(dst, bank[:, :].rearrange("p (t a q) -> p t a q", t=2, a=KD)).then_inc(ring_read, 1)
                elif kind == "gate":
                    _, c, half = e
                    if (c, half) == (0, 0):
                        dve.wait_ge(ld["bg"], 16)
                    dve.tensor_tensor(gate_sb[:, c, CH * half:CH * (half + 1)].rearrange("p (t d) -> p t d", t=2),
                                      bank[:, :].rearrange("p (t d) -> p t d", t=2),
                                      bg_sb[:, :].unsqueeze(1).to_broadcast([P, 2, D]), ALU.add).then_inc(ring_read, 1)
                elif kind == "mx":
                    _, n, k = e
                    qt, h, k0, w, _, slot = max_pieces(n)[k]
                    dve.tensor_reduce(pmax[:, n % 2, qt, h, slot:slot + 1], bank[:, 0:w], AX_X,
                                      ALU.max).then_inc(ring_read, 1)
                elif kind == "mred":
                    n = e[1]
                    dve.wait_ge(ring_read, ring_at[("mx", n, len(max_pieces(n)) - 1)] + 1)
                    if n >= 2:
                        dve.wait_ge(nm_ready, n - 1)
                    dve.tensor_reduce(rmax[:, n % 2, :], pmax[:, n % 2, :, :, :].rearrange("p t h k -> p (t h) k"), AX_X,
                                      ALU.max).then_inc(mx_reduced, 1)
                elif kind == "mT":
                    n = e[1]
                    if n >= 2:
                        dve.wait_ge(m_landed[(n - 2) % 4], 32 * ((n - 2) // 4 + 1))
                    dve.tensor_copy(m_row[:, n % 2, :], bank[0:8, 0:CH // 2].bitcast(BF16)).then_inc(ring_read, 1)
                elif kind == "oT":
                    n = e[1]
                    c, g = n // G, n % G
                    view = bank[:, :].rearrange("p (t h w) -> p t h w", t=TPC, h=4)
                    step(dve.tensor_scalar(rsum[:, :, :], view[:, :, :, DK], TINY, None, ALU.max))
                    step(dve.reciprocal(rinv[:, :, :], rsum[:, :, :]))
                    if g == 0 and c:
                        dve.wait_ge(side_full, side_at[("gT", c - 1, 1)] + 1)
                    dve.tensor_tensor(att_sb[:, :, 64 * g:64 * (g + 1)].rearrange("p t (h d) -> p t h d", h=4),
                                      view[:, :, :, 0:DK], rinv[:, :, :].unsqueeze(3).to_broadcast([P, TPC, 4, DK]),
                                      ALU.mult).then_inc(ring_read, 1)
                elif kind == "wo":
                    _, c, half = e
                    t0 = TPC * c + 2 * half
                    view = x_sb[:, t0:t0 + 2, :]
                    dve.tensor_tensor(view, bank[:, :].rearrange("p (t d) -> p t d", t=2), view,
                                      ALU.add).then_inc(ring_read, 1)
                elif kind == "logits":
                    c = e[1]
                    view = bank[:, 0:TPC * E].rearrange("p (t e) -> p t e", t=TPC)
                    step(dve.tensor_reduce(r_max[:, :], view, AX_X, ALU.max))
                    dve.tensor_tensor(r_log[:, :, :], view, r_max[:, :].unsqueeze(2).to_broadcast([P, TPC, E]),
                                      ALU.subtract).then_inc(r_log_ready, 1)
                    dve.wait_ge(r_log_ready, c + 1)
                    dve.memset(r_sum[:, :], 0.0).then_inc(ring_read, 1)
                elif kind == "rank0":
                    c = e[1]
                    dve.wait_ge(r_exp_ready, c + 1)
                    dve.wait_ge(ring_read, ring_at[("logits", c)] + 1)
                    step(dve.tensor_reduce(r_sum[:, :], r_exp[:, :, :], AX_X, ALU.add))
                    step(dve.reciprocal(r_inv[:, :], r_sum[:, :]))
                    step(dve.tensor_tensor(r_prob[:, :, :], r_exp[:, :, :],
                                           r_inv[:, :].unsqueeze(2).to_broadcast([P, TPC, E]), ALU.mult))
                elif kind == "rank1":
                    c = e[1]
                    dve.wait_ge(ring_full, ring_at[("wo", c, 1)] + 1)
                    four = [P, TPC, E, E]
                    other = r_prob[:, :, :].unsqueeze(2).to_broadcast(four)
                    own = r_prob[:, :, :].unsqueeze(3).to_broadcast(four)
                    dve.tensor_tensor(r_gt[:, :, :, :], other, own, ALU.is_gt).then_inc(dve_step, 1)
                    dve.tensor_tensor(r_eq[:, :, :, :], other, own, ALU.is_equal).then_inc(dve_step, 1)
                    steps[0] += 2
                    dve.wait_ge(dve_step, steps[0])
                elif kind == "rank":
                    c = e[1]
                    four = [P, TPC, E, E]
                    dve.wait_ge(consts, 8)
                    step(dve.tensor_tensor(r_eq[:, :, :, :], r_eq[:, :, :, :],
                                           lower[:, :, :].unsqueeze(1).to_broadcast(four), ALU.mult))
                    step(dve.tensor_tensor(r_gt[:, :, :, :], r_gt[:, :, :, :], r_eq[:, :, :, :], ALU.add))
                    step(dve.tensor_reduce(r_rank[:, :, :], r_gt[:, :, :, :], AX_X, ALU.add))
                    if c:
                        dve.wait_ge(ring_full, ring_at[("sT", c - 1)] + 1)
                    dve.scalar_tensor_tensor(out=scale_sb[:, :, :], in0=r_rank[:, :, :], scalar=1.5,
                                             in1=r_prob[:, :, :], op0=ALU.is_lt, op1=ALU.mult).then_inc(scale_ready, 1)
                elif kind == "sT":
                    c = e[1]
                    if c:
                        dve.wait_ge(s_stored[c - 1], 16)
                    dve.tensor_copy(sT_sb[:, :], bank[0:E, :]).then_inc(ring_read, 1)
                elif kind == "ws":
                    ex = e[1]
                    if ex == 0:
                        for name, times in (("w1", KD), ("w3", KD), ("w2", 1)):
                            dve.wait_ge(ld[name], 16 * times)
                        dve.wait_ge(side_full, st_at[(last_unit[NC * G - 2], 3)] + 1)
                    if ex < EARLY_WS:
                        dve.tensor_copy(w_hi[:, ex, :, :], w_sb[:, ex, :, :]).then_inc(w_hi_ready, 1)
                    dve.wait_ge(w_hi_ready, ex + 1)
                    dve.tensor_tensor(w_lo[:, ex, :, :], w_sb[:, ex, :, :], w_hi[:, ex, :, :], ALU.subtract).then_inc(w_lo_ready, 1)
                elif kind == "xs":
                    c = e[1]
                    if c == 0:
                        dve.wait_ge(*taken(("xT1", c, 1)))
                        dve.wait_ge(ld["w2"], 16)
                        dve.tensor_copy(x_hi[:, c % 2, :, :], gate_sb[:, c, :].rearrange("p (a q) -> p a q", a=KD)
                                        ).then_inc(x_hi_ready, 1)
                    dve.wait_ge(x_hi_ready, c + 1)
                    dve.tensor_tensor(x_lo[c % 2][:, :, :], gate_sb[:, c, :].rearrange("p (a q) -> p a q", a=KD),
                                      x_hi[:, c % 2, :, :], ALU.subtract).then_inc(x_lo_ready, 1)
                elif kind == "a":
                    _, c, ex = e
                    i = c * E + ex
                    if i == 0:
                        dve.wait_ge(pv_done, len(units))
                    if ex == 0:
                        dve.wait_ge(s_landed[c], 16)
                    if i >= 2:
                        dve.wait_ge(h_ready, i - 1)
                    dve.tensor_tensor(u_sb[:, i % 2, :], bank[:, :], scale_bc[c % 2][:, ex, :], ALU.mult).then_inc(ring_read, 1)
                elif kind == "b":
                    _, c, ex = e
                    i = c * E + ex
                    if i >= 2:
                        dve.wait_ge(h_lo_ready, i - 1)
                    dve.tensor_tensor(v_sb[:, i % 2, :], bank[:, :], scale_bc[c % 2][:, ex, :], ALU.mult).then_inc(ring_read, 1)
                elif kind == "h":
                    _, c, ex = e
                    i = c * E + ex
                    dve.wait_ge(silu_done, i + 1)
                    dve.wait_ge(ring_read, ring_at[("b", c, ex)] + 1)
                    dve.tensor_tensor(v_sb[:, i % 2, :], u_sb[:, i % 2, :], v_sb[:, i % 2, :], ALU.mult).then_inc(h_ready, 1)
                elif kind == "hl":
                    _, c, ex = e
                    i = c * E + ex
                    dve.wait_ge(h_hi_ready, i + 1)
                    dve.tensor_tensor(h_lo[:, i % 2, :], v_sb[:, i % 2, :], h_hi[:, i % 2, :], ALU.subtract).then_inc(h_lo_ready, 1)
                elif kind == "out":
                    c = e[1]
                    dve.wait_ge(y_full, E * (c + 1))
                    for t in range(TPC):
                        view = x_sb[:, TPC * c + t, :]
                        last = dve.tensor_tensor(view, psum[Y_BANKS[t]][:, 0:D], view, ALU.add)
                    last.then_inc(y_added, 1)

        @block.tensor
        def _(pe):
            def make(e):
                if places[e][1]:
                    pe.wait_ge(ring_read, places[e][1])
                return ring_bank(e)

            def make_side(e):
                i = side_at[e]
                if i >= ST_BANKS:
                    pe.wait_ge(side_read, i - ST_BANKS + 1)
                return side_bank(e)

            def contract(dst, lhs, rhs):
                for a in range(KD):
                    last = pe.matmul(dst, lhs(a), rhs(a), start=(a == 0), stop=(a == KD - 1))
                return last

            for e in plan:
                kind = e[0]
                if kind == "kq":
                    _, what, m, c = e
                    w = min(CH, KEYS - CH * c) if what == "k" else CH
                    if what == "k":
                        if c == 0:
                            pe.wait_ge(ld["wk"], 16)
                        pe.wait_ge(ld_ctx[c], 16)
                        wt, moving = wk_sb, ctx_sb[:, :, CH * c:CH * c + w]
                    else:
                        if c == 0:
                            pe.wait_ge(ld["wq"], 16)
                        pe.wait_ge(side_read, side_at[("xT0", c, 1)] + 1)
                        wt, moving = wq_sb, xn_t[:, :, :]
                    bank = make_side(e)
                    contract(bank[:, 0:w], lambda a: wt[:, a, P * m:P * (m + 1)],
                             lambda a: moving[:, a, :]).then_inc(side_full, 1)
                elif kind == "v":
                    t = e[1]
                    r = key_rows(t)
                    if t == 0:
                        pe.wait_ge(ld["wv"], 16)
                    bank = make_side(e)
                    contract(bank[0:r, 0:D], lambda a: ctx_sb[:, a, P * t:P * t + r],
                             lambda a: wv_sb[:, a, :]).then_inc(side_full, 1)
                elif kind in ("xT0", "xT1"):
                    _, c, half = e
                    first = kind == "xT0"
                    if first and c == 0:
                        pe.wait_ge(consts, 8)
                    pe.wait_ge(xn_ready, norm_at[(0 if first else 1, c)] + 1)
                    bank = make_side(e) if by_side(e) else make(e)
                    for t in range(2):
                        for a in range(KD):
                            last = pe.transpose(bank[:, P * (2 * t + a):P * (2 * t + a + 1)],
                                                xn_sb[:, 2 * half + t, P * a:P * (a + 1)], ident[:, :])
                    last.then_inc(side_full if by_side(e) else ring_full, 1)
                elif kind == "gate":
                    _, c, half = e
                    if (c, half) == (0, 0):
                        pe.wait_ge(ld["wg"], 16)
                    bank = make(e)
                    for t in range(2):
                        tile = P * (2 * half + t)
                        last = contract(bank[:, D * t:D * (t + 1)], lambda a: xn_t[:, a, tile:tile + P],
                                        lambda a: wg_sb[:, a, :])
                    last.then_inc(ring_full, 1)
                elif kind == "mx":
                    _, n, k = e
                    c, g = n // G, n % G
                    qt, h, k0, w, diagonal, _ = max_pieces(n)[k]
                    if k == 0:
                        if g == 0:
                            pe.wait_ge(q_landed[c], 16 * len(Q_PARTS))
                            pe.wait_ge(k_landed[c], 16 * len(K_PARTS))
                        if n == 0:
                            pe.wait_ge(bias_landed, 16)
                            pe.wait_ge(aug_q, 16)
                    bank = make(e)
                    d = P * (TPC * c + qt) - k0
                    for b0 in range(0, w, CH):
                        b1 = min(b0 + CH, w)
                        cut = diagonal and b0 <= d < b1
                        last = pe.matmul(bank[:, b0:b1], qaug[0:ROW_MAX, c % 2, 4 * g + h, P * qt:P * (qt + 1)],
                                         kaug[0:ROW_MAX, 4 * g + h, k0 + b0:k0 + b1], start=True, stop=not cut)
                        if cut:
                            last = pe.matmul(bank[:, d:b1], ident_b[:, :], tri_qk[:, 0:b1 - d], start=False, stop=True)
                    last.then_inc(ring_full, 1)
                elif kind == "mT":
                    n = e[1]
                    pe.wait_ge(nm_ready, n + 1)
                    bank = make(e)[0:8, 0:CH // 2].bitcast(BF16)
                    for t in range(TPC):
                        last = pe.transpose(bank[:, P * t:P * (t + 1)],
                                            nmax_b[:, n % 2, t, :, :].rearrange("p a h -> p (a h)"), ident_b[:, :])
                    last.then_inc(ring_full, 1)
                elif kind == "st":
                    _, u, n, j, h = e
                    c, g = n // G, n % G
                    i = st_at[(u, h)]
                    off = max(0, P * (j - TPC * c))
                    r = key_rows(j)
                    if j == 0 and h == 0:
                        pe.wait_ge(m_landed[n % 4], 32 * (n // 4 + 1))
                    bank = make_side(e)
                    diagonal = j >= TPC * c
                    last = pe.matmul(bank[0:r, off:CH], kaug[0:ROWS, 4 * g + h, P * j:P * j + r],
                                     qaug[0:ROWS, c % 2, 4 * g + h, off:CH], start=True, stop=not diagonal)
                    if diagonal:
                        last = pe.matmul(bank[0:r, off:off + P], tri_qk[:, 0:r], ident_b[:, :], start=False, stop=True)
                    last.then_inc(side_full, 1)
                elif kind == "pv":
                    _, u, n, j = e
                    c, g = n // G, n % G
                    off = max(0, P * (j - TPC * c))
                    r = key_rows(j)
                    if j == 0 and n >= 1:
                        pe.wait_ge(o_copied, n)
                    pe.wait_ge(side_read, st_at[(u, 3)] + 1)
                    for h in range(4):
                        col = (j * H + 4 * g + h) * VW
                        last = pe.matmul(psum[O_BANK][32 * h:32 * h + 32, off:CH], vaug[0:r, col:col + 32],
                                         probs[0:r, u % NSLOT, h, off:CH], start=(j == 0), stop=(j == key_tiles(c) - 1))
                    last.then_inc(pv_done, 1)
                elif kind == "oT":
                    n = e[1]
                    pe.wait_ge(o_copied, n + 1)
                    bank = make(e)
                    for t in range(TPC):
                        last = pe.transpose(bank[:, P * t:P * (t + 1)], o_sb[:, P * t:P * (t + 1)], ident[:, :])
                    last.then_inc(ring_full, 1)
                elif kind == "gT":
                    _, c, half = e
                    pe.wait_ge(gated, G * (c + 1))
                    bank = make_side(e) if by_side(e) else make(e)
                    for t in range(2):
                        for a in range(KD):
                            last = pe.transpose(bank[:, P * (2 * t + a):P * (2 * t + a + 1)],
                                                att_sb[:, 2 * half + t, P * a:P * (a + 1)], ident[:, :])
                    last.then_inc(side_full if by_side(e) else ring_full, 1)
                elif kind == "wo":
                    _, c, half = e
                    if (c, half) == (0, 0):
                        pe.wait_ge(ld["wo"], 16)
                    pe.wait_ge(*taken(("gT", c, half)))
                    bank = make(e)
                    for t in range(2):
                        tile = P * (2 * half + t)
                        last = contract(bank[:, D * t:D * (t + 1)], lambda a: att_t[:, a, tile:tile + P],
                                        lambda a: wo_sb[:, a, :])
                    last.then_inc(ring_full, 1)
                elif kind == "logits":
                    c = e[1]
                    if c == 0:
                        pe.wait_ge(ld["gw"], 16)
                    pe.wait_ge(*taken(("xT1", c, 1)))
                    bank = make(e)
                    for t in range(TPC):
                        tile = P * t
                        last = contract(bank[:, E * t:E * (t + 1)], lambda a: gate_sb[:, c, CH * a + tile:CH * a + tile + P],
                                        lambda a: gw_sb[:, a, :])
                    last.then_inc(ring_full, 1)
                elif kind == "sT":
                    c = e[1]
                    pe.wait_ge(scale_ready, c + 1)
                    bank = make(e)
                    for t in range(TPC):
                        last = pe.transpose(bank[0:E, P * t:P * (t + 1)], scale_sb[:, t, :], ident[:, :])
                    last.then_inc(ring_full, 1)
                elif kind in ("a", "b"):
                    _, c, ex = e
                    if kind == "a":
                        if c == 0:
                            pe.wait_ge(w_lo_ready, ex + 1)
                        if ex == 0:
                            pe.wait_ge(x_lo_ready, c + 1)
                    part = 0 if kind == "a" else 1
                    bank = make(e)
                    for a in range(KD):
                        hi, lo = (w[:, ex, part, HID * a:HID * (a + 1)] for w in (w_hi, w_lo))
                        pe.matmul(bank[:, :], hi, x_hi[:, c % 2, a, :], start=(a == 0), stop=False)
                        pe.matmul(bank[:, :], hi, x_lo[c % 2][:, a, :], start=False, stop=False)
                        last = pe.matmul(bank[:, :], lo, x_hi[:, c % 2, a, :], start=False, stop=(a == KD - 1))
                    last.then_inc(ring_full, 1)
                elif kind == "y":
                    _, c, ex = e
                    i = c * E + ex
                    if i == 0:
                        pe.wait_ge(side_read, len(side_at))
                        pe.wait_ge(o_copied, NC * G)
                    if ex == 0 and c:
                        pe.wait_ge(y_added, c)
                    pe.wait_ge(h_lo_ready, i + 1)
                    for t in range(TPC):
                        dst = psum[Y_BANKS[t]][:, 0:D]
                        hi, lo = (h[:, i % 2, P * t:P * (t + 1)] for h in (h_hi, h_lo))
                        pe.matmul(dst, hi, w_hi[:, ex, 2, :], start=(ex == 0), stop=False)
                        pe.matmul(dst, hi, w_lo[:, ex, 2, :], start=False, stop=False)
                        last = pe.matmul(dst, lo, w_hi[:, ex, 2, :], start=False, stop=(ex == E - 1))
                    last.then_inc(y_full, 1)


def kernel(x, ctx_1024, mask_BxS2_ik0, L0_xattn_Wq, L0_xattn_Wk, L0_xattn_Wv, L0_xattn_Wo, L0_xattn_Wg, L0_xattn_bg,
           L0_ffn_gate_w, L0_ffn_w1, L0_ffn_w2, L0_ffn_w3):
    import concourse.bacc as bacc
    from concourse.bass_utils import run_bass_kernel_spmd

    x, ctx_1024 = np.asarray(x), np.asarray(ctx_1024)
    arrays = {
        "x": x.reshape(TOK, D),
        "ctx_t": ctx_1024.reshape(KEYS, D).T,
        "mask": np.asarray(mask_BxS2_ik0).reshape(1, KEYS),
        "wq_t": np.asarray(L0_xattn_Wq).T,
        "wk_t": np.asarray(L0_xattn_Wk).T,
        "wv_t": np.asarray(L0_xattn_Wv).T,
        "wo_t": np.asarray(L0_xattn_Wo).T,
        "wg_t": np.asarray(L0_xattn_Wg).T,
        "bg": np.asarray(L0_xattn_bg),
        "gate_w": np.asarray(L0_ffn_gate_w),
        "w1": np.asarray(L0_ffn_w1),
        "w2": np.asarray(L0_ffn_w2),
        "w3": np.asarray(L0_ffn_w3),
    }
    arrays = {f"in_{k}": np.ascontiguousarray(a) for k, a in arrays.items()}
    nc = bacc.Bacc("TRN2", target_bir_lowering=False, num_devices=1)
    args = [nc.dram_tensor(k, a.shape, mybir.dt.from_np(a.dtype), kind="ExternalInput").ap() for k, a in arrays.items()]
    out = nc.dram_tensor("out", (TOK, D), F32, kind="ExternalOutput").ap()
    build(nc, *args, out)
    r = run_bass_kernel_spmd(nc, [arrays], core_ids=[0])
    return r.results[0]["out"].reshape(1, TOK, D)
```
